# Optimizing a Trainium2 kernel written in Bass

```python
import numpy as np
import jax
import jax.numpy as jnp

def _softmax(x, axis=-1):
    return jax.nn.softmax(x, axis=axis)

def _gelu(x):
    return jax.nn.gelu(x, approximate=True)

def _silu(x):
    return jax.nn.silu(x)

def _sigmoid(x):
    return jax.nn.sigmoid(x)

def _layernorm(x, axis=-1, eps=1e-05):
    m = jnp.mean(x, axis=axis, keepdims=True)
    v = jnp.var(x, axis=axis, keepdims=True)
    return (x - m) / jnp.sqrt(v + eps)

def _scatter_add(tgt, idx, src, axis=0):
    return tgt.at[idx].add(src)

def _segment_sum(src, seg, n):
    return jax.ops.segment_sum(src, seg, n)
kernel_name = 'mk_flamingo_gated_d1_seqx_r4_38d104'

def setup_inputs(seed: int=0):
    np.random.seed(seed)
    _w = jnp.asarray

    def _rec_inputs():
        import jax
        import jax.numpy as jnp
        _rk = jax.random.key(seed)
        x = -0.000125 + 0.9999 * jax.random.normal(jax.random.fold_in(_rk, 1), (32, 128, 512), jnp.float32)
        _lenS = 128 - jax.random.randint(jax.random.fold_in(_rk, 7), (32,), 0, max(1, 128 // 4) + 1, jnp.int32)
        _lenS2 = 128 - jax.random.randint(jax.random.fold_in(_rk, 8), (32,), 0, max(1, 128 // 4) + 1, jnp.int32)
        _ctx_2048P = jax.random.normal(jax.random.fold_in(_rk, 11), (32, 16, 512), jnp.float32)
        _ctx_2048c = jax.random.dirichlet(jax.random.fold_in(_rk, 511), 0.3 * jnp.ones((16,), jnp.float32), (32, 128))
        _ctx_2048t = jnp.einsum('bsk,bkd->bsd', _ctx_2048c, _ctx_2048P)
        _ctx_2048t = _ctx_2048t * jax.lax.rsqrt(jnp.mean(jnp.square(_ctx_2048t)) + 1e-12) * 0.953939
        ctx_2048 = -0.000514642 + 1.00011 * (_ctx_2048t + 0.3 * jax.random.normal(jax.random.fold_in(_rk, 611), (32, 128, 512), jnp.float32))
        _validS = jnp.arange(128)[None, :] < _lenS[:, None]
        _validS2 = jnp.arange(128)[None, :] < _lenS2[:, None]
        _causal = jnp.tril(jnp.ones((128, 128), dtype=bool))
        mask_BxS2_bk0 = jnp.logical_not(jnp.broadcast_to(_validS2[:, :], (32, 128)))
        _g = jax.random.normal(jax.random.fold_in(_rk, 9001), (2, 1), jnp.float32)
        _g = jnp.sign(_g) * jnp.maximum(jnp.abs(_g), 1.0) + (_g == 0) * 1.0
        g_xattn = _g[0]
        g_ffn = _g[1]
        return (x, ctx_2048, mask_BxS2_bk0, g_xattn, g_ffn)
    x, ctx_2048, mask_BxS2_bk0, g_xattn, g_ffn = _rec_inputs()

    def _L0_xattn_setup():
        import jax, jax.numpy as jnp
        import numpy as np
        key = jax.random.key(seed)
        k1, k2, k3 = jax.random.split(key, 3)
        B, S, D, M = (8, 512, 512, 128)
        hidden_states = jax.random.normal(k1, (B, S, D), dtype=jnp.float32)
        memory_tokens = jax.random.normal(k2, (B, M, D), dtype=jnp.float32)
        memory_mask = jax.random.randint(k3, (B, M), 0, 2).astype(jnp.bool_)
        return {'hidden_states': hidden_states, 'memory_tokens': memory_tokens, 'memory_mask': memory_mask}
    _L0_xattn_all = _L0_xattn_setup()
    _L0_xattn_in = {k: v for k, v in _L0_xattn_all.items() if k in ()}
    del _L0_xattn_all

    def _L0_ffn_setup():
        import jax, jax.numpy as jnp
        import numpy as np

        def _sparsify_2to4(h):
            B, S, I = h.shape
            g = h.reshape(B, S, I // 4, 4)
            a = jnp.abs(g)
            _, idx = jax.lax.top_k(a, 2)
            pos = jnp.arange(4)
            mask = (pos == idx[..., 0:1]) | (pos == idx[..., 1:2])
            return (g * mask.astype(g.dtype)).reshape(B, S, I)
        key = jax.random.key(seed)
        k1, k2, k3, k4 = jax.random.split(key, 4)
        B, S, H, I = (4, 512, 512, 2048)
        x = jax.random.normal(k1, (B, S, H), dtype=jnp.float32)
        w_gate = jax.random.normal(k2, (H, I), dtype=jnp.float32) / np.sqrt(H)
        w_up = jax.random.normal(k3, (H, I), dtype=jnp.float32) / np.sqrt(H)
        w_down = jax.random.normal(k4, (I, H), dtype=jnp.float32) / np.sqrt(I)
        return {'x': x, 'w_gate': w_gate, 'w_up': w_up, 'w_down': w_down}
    _L0_ffn_all = _L0_ffn_setup()
    _L0_ffn_in = {k: v for k, v in _L0_ffn_all.items() if k in ('w_gate', 'w_up', 'w_down')}
    del _L0_ffn_all
    return {'x': x, 'ctx_2048': ctx_2048, 'mask_BxS2_bk0': mask_BxS2_bk0, 'g_xattn': g_xattn, 'g_ffn': g_ffn, 'L0_ffn_w_gate': _L0_ffn_in['w_gate'], 'L0_ffn_w_up': _L0_ffn_in['w_up'], 'L0_ffn_w_down': _L0_ffn_in['w_down']}

def reference(x, ctx_2048, mask_BxS2_bk0, g_xattn, g_ffn, L0_ffn_w_gate, L0_ffn_w_up, L0_ffn_w_down):
    import jax
    import jax.numpy as jnp

    def _L0_xattn_ref(hidden_states, memory_tokens, memory_mask):
        import jax, jax.numpy as jnp
        import numpy as np
        B, S, D = hidden_states.shape
        scale = 1.0 / jnp.sqrt(jnp.asarray(D, hidden_states.dtype))
        scores = jnp.einsum('bsd,bmd->bsm', hidden_states, memory_tokens) * scale
        neg_inf = jnp.asarray(-1e+30, scores.dtype)
        scores = jnp.where(memory_mask[:, None, :], scores, neg_inf)
        attn = jax.nn.softmax(scores, axis=-1)
        readout = jnp.einsum('bsm,bmd->bsd', attn, memory_tokens)
        valid_b = jnp.any(memory_mask, axis=-1)
        out = jnp.where(valid_b[:, None, None], readout, jnp.zeros_like(readout))
        return out

    def _L0_ffn_ref(x, w_gate, w_up, w_down):
        import jax, jax.numpy as jnp
        import numpy as np

        def _sparsify_2to4(h):
            B, S, I = h.shape
            g = h.reshape(B, S, I // 4, 4)
            a = jnp.abs(g)
            _, idx = jax.lax.top_k(a, 2)
            pos = jnp.arange(4)
            mask = (pos == idx[..., 0:1]) | (pos == idx[..., 1:2])
            return (g * mask.astype(g.dtype)).reshape(B, S, I)
        h = jax.nn.silu(jnp.einsum('bsh,hi->bsi', x, w_gate)) * jnp.einsum('bsh,hi->bsi', x, w_up)
        h_sparse = _sparsify_2to4(h)
        return jnp.einsum('bsi,ih->bsh', h_sparse, w_down)
    x = x + jnp.tanh(g_xattn[0]) * _L0_xattn_ref(_layernorm(x, axis=-1), ctx_2048, mask_BxS2_bk0)
    x = x + jnp.tanh(g_ffn[0]) * _L0_ffn_ref(_layernorm(x, axis=-1), L0_ffn_w_gate, L0_ffn_w_up, L0_ffn_w_down)
    return x

_drawn_inputs = setup_inputs


def setup_inputs(seed=0):
    import zlib

    import numpy as np

    out = dict(_drawn_inputs(seed))
    spreads = {}
    factors = {}
    for name, (base, spread) in spreads.items():
        noise = np.random.default_rng([zlib.crc32(name.encode()), seed]).standard_normal(out[name].shape)
        drawn = base * np.exp(spread * noise) if base else spread * noise
        out[name] = jnp.asarray(drawn.astype(out[name].dtype))
    for name, factor in factors.items():
        out[name] = (out[name] * factor).astype(out[name].dtype)
    return out
```

```python
from contextlib import ExitStack

import concourse.bass as bass
from concourse import mybir

F32 = mybir.dt.float32
F32R = mybir.dt.float32r
BF16 = mybir.dt.bfloat16
U8 = mybir.dt.uint8
ALU = mybir.AluOpType
ACT = mybir.ActivationFunctionType
AX = mybir.AxisListType

P = 128
B, S, D = 32, 128, 512
M = 128
I = 2048
KC = D // P
GROUP = 4
PASSES = I // (P * GROUP)
IQ = I // PASSES
ROWS = 512
TILES = ROWS // P
BLOCKS = B * S // ROWS
EPS = 1e-5
SCALE = float(D) ** -0.5
BIG = 1e30
RING = 8
LAST_LAG = 7
KEEP = {0: (2, ALU.is_ge, 2.0), 1: (0, ALU.is_ge, 1.0), 2: (1, ALU.is_le, 0.0), 3: (3, ALU.is_le, 1.0)}
PAIR = {(0, 1): 0, (2, 3): 1, (1, 3): 2, (0, 2): 3, (1, 2): 4, (0, 3): 5}


def wait(engine, semaphore, value):
    if not isinstance(value, int) or value > 0:
        engine.wait_ge(semaphore, value)


def wait_apart(engine, semaphore, value, started):
    if isinstance(value, int):
        wait(engine, semaphore, value)
        return
    engine.compute_val(value)
    engine.wait_ge(started, 1)
    engine.wait_ge(semaphore, value)


def flamingo_gated(nc, x, ctx, mask, g_xattn, g_ffn, w_gate, w_up, w_down, out):
    xnT_dram = nc.dram_tensor("xnT_scratch", [BLOCKS, P, KC, ROWS], F32).ap()
    gate_view = w_gate.rearrange("(c p) i -> p c i", p=P)
    up_view = w_up.rearrange("(c p) i -> p c i", p=P)
    down_view = w_down.rearrange("(q p j) n -> q p (j n)", p=P, j=GROUP)
    x_view = x.rearrange("b s d -> s b d")
    out_view = out.rearrange("b s d -> s b d")

    whole = ExitStack()
    with whole:
        def sb(name, shape, dtype, scope=whole):
            return scope.enter_context(nc.sbuf_tensor(name, shape, dtype))

        def sem(name, scope=whole):
            return scope.enter_context(nc.semaphore(name))

        rows = sb("rows", [P, B * D], F32)
        gu_hi = sb("gu_hi", [P, 2, GROUP, KC, P], F32R)
        gu_lo = sb("gu_lo", [P, 2, GROUP, KC, P], F32R)
        dn_hi = sb("dn_hi", [P, GROUP, D], F32R)
        dn_lo = sb("dn_lo", [P, GROUP, D], F32R)
        gu_raw = sb("gu_raw", [P, 2, KC, IQ], F32)
        dn_raw = gu_raw[:, 0, :, :]
        ffn_gate = sb("ffn_gate", [P, 1], F32)

        gate_raw_loaded, up_raw_loaded, dn_raw_loaded = sem("gate_raw_loaded"), sem("up_raw_loaded"), sem("dn_raw_loaded")
        gu_hi_done, gu_lo_done = sem("gu_hi_done"), sem("gu_lo_done")
        dn_hi_done, dn_lo_done = sem("dn_hi_done"), sem("dn_lo_done")

        def gu_raw_of(g, j):
            return gu_raw[:, g, :, j:IQ:GROUP]

        def split_gu_hi(act, q, j):
            act.wait_ge(gate_raw_loaded, 16 * (q + 1))
            act.wait_ge(up_raw_loaded, 16 * (q + 1))
            for g in range(2):
                nc.scalar.activation(gu_hi[:, g, j], gu_raw_of(g, j), ACT.Copy).then_inc(gu_hi_done, 1)

        def split_gu_lo(dve, q, j):
            for g in range(2):
                dve.wait_ge(gu_hi_done, 2 * GROUP * q + 2 * j + g + 1)
                nc.vector.tensor_tensor(gu_lo[:, g, j], gu_raw_of(g, j), gu_hi[:, g, j].bitcast(F32),
                                        ALU.subtract).then_inc(gu_lo_done, 1)

        def split_dn_hi(act, q, j):
            act.wait_ge(dn_raw_loaded, 16 * (q + 1))
            nc.scalar.activation(dn_hi[:, j], dn_raw[:, j], ACT.Copy).then_inc(dn_hi_done, 1)

        def split_dn_lo(dve, q, j):
            dve.wait_ge(dn_hi_done, GROUP * q + j + 1)
            nc.vector.tensor_tensor(dn_lo[:, j], dn_raw[:, j], dn_hi[:, j].bitcast(F32),
                                    ALU.subtract).then_inc(dn_lo_done, 1)

        attention(nc, sb, sem, locals())
        feed_forward(nc, sb, sem, locals())


def attention(nc, sb, sem, shared):
    x, ctx, mask, g_xattn, g_ffn = (shared[n] for n in ("x", "ctx", "mask", "g_xattn", "g_ffn"))
    rows, gu_raw, dn_raw, ffn_gate = (shared[n] for n in ("rows", "gu_raw", "dn_raw", "ffn_gate"))
    x_view, xnT_dram = shared["x_view"], shared["xnT_dram"]
    gate_view, up_view, down_view = shared["gate_view"], shared["up_view"], shared["down_view"]
    gate_raw_loaded, up_raw_loaded, dn_raw_loaded = (shared[n] for n in ("gate_raw_loaded", "up_raw_loaded", "dn_raw_loaded"))
    gu_lo_done = shared["gu_lo_done"]
    split_gu_hi, split_gu_lo, split_dn_hi, split_dn_lo = (
        shared[n] for n in ("split_gu_hi", "split_gu_lo", "split_dn_hi", "split_dn_lo"))

    scope = ExitStack()
    with scope:
        def sbuf(name, shape, dtype=F32):
            return sb(name, shape, dtype, scope)

        def psum(name, shape):
            return scope.enter_context(nc.psum_tensor(name, shape, F32))

        def semaphore(name):
            return sem(name, scope)

        x_in = sbuf("x_in", [P, RING, D])
        ctx_in = sbuf("ctx_in", [P, RING, D])
        xn = sbuf("xn", [P, 2, D])
        xnT = sbuf("xnT", [P, 2, KC, P])
        ctxT = sbuf("ctxT", [P, 2, KC, P])
        mask_in = sbuf("mask_in", [P, B * M], U8)
        mask_neg = sbuf("mask_neg", [P, B * M], BF16)
        neg_scores = sbuf("neg_scores", [P, 2, M])
        neg_max = sbuf("neg_max", [P, RING])
        probs = sbuf("probs", [P, 2, M])
        probsT = sbuf("probsT", [P, 2, P])
        prob_sum = sbuf("prob_sum", [P, RING])
        out_scale = sbuf("out_scale", [P, RING])
        x1n = sbuf("x1n", [P, 2, D])
        x1nT = sbuf("x1nT", [P, TILES, KC, P])
        bn6 = sbuf("bn6", [P, 2, 2, 6])
        bn_mv = sbuf("bn_mv", [P, 2, RING, 2])
        var_eps = sbuf("var_eps", [P, 2, RING])
        rstd = sbuf("rstd", [P, 2, RING])
        minus_half = sbuf("minus_half", [P, 1])
        xattn_gate = sbuf("xattn_gate", [P, 1])
        gates_in = sbuf("gates_in", [P, 2])
        valid = sbuf("valid", [P, B])
        gate_valid = sbuf("gate_valid", [P, B])
        ident = sbuf("ident", [P, P])

        ps_xT = psum("ps_xT", [P, KC, P])
        ps_cT = psum("ps_cT", [P, KC, P])
        ps_sc = [psum(f"ps_sc{i}", [P, 512]) for i in range(2)]
        ps_pT = psum("ps_pT", [P, 512])
        ps_av = [psum(f"ps_av{i}", [P, D]) for i in range(2)]
        ps_nT = psum("ps_nT", [P, KC, P])

        in_loaded = [semaphore(f"in_loaded{k}") for k in range(RING)]
        consts_loaded = semaphore("consts_loaded")
        ident_set, ident_done, half_done = semaphore("ident_set"), semaphore("ident_done"), semaphore("half_done")
        gates_done, valid_done, gate_valid_done = semaphore("gates_done"), semaphore("valid_done"), semaphore("gate_valid_done")
        bn1_done, stats1_done = semaphore("bn1_done"), semaphore("stats1_done")
        bn2_done, stats2_done = semaphore("bn2_done"), semaphore("stats2_done")
        var_eps_done = [semaphore(f"var_eps{i}_done") for i in (1, 2)]
        rstd_done = [semaphore(f"rstd{i}_done") for i in (1, 2)]
        mask_neg_done, xn_done, x1n_done = semaphore("mask_neg_done"), semaphore("xn_done"), semaphore("x1n_done")
        xT_done, cT_done, xT_copied, cT_copied = (semaphore(n) for n in ("xT_done", "cT_done", "xT_copied", "cT_copied"))
        scores_done, neg_scores_done, neg_max_done = semaphore("scores_done"), semaphore("neg_scores_done"), semaphore("neg_max_done")
        probs_done, pT_done, pT_copied = semaphore("probs_done"), semaphore("pT_done"), semaphore("pT_copied")
        av_done, scale_step, x1_done = semaphore("av_done"), semaphore("scale_step"), semaphore("x1_done")
        nT_done, nT_copied = semaphore("nT_done"), semaphore("nT_copied")
        xnT_stored = [semaphore(f"xnT_stored{k}") for k in range(TILES)]

        def slots(engine, slot):
            def at_of(it, k):
                def at(lag):
                    r, kk = it + (k - lag) // RING, (k - lag) % RING
                    if isinstance(r, int) and not 0 <= r < B // RING:
                        return None
                    return r, kk
                return at
            for k in range(RING):
                slot(at_of(0, k), 0, k)
            with engine.Fori(1, B // RING) as it:
                for k in range(RING):
                    slot(at_of(it, k), None, k)
            for k in range(LAST_LAG):
                slot(at_of(B // RING, k), B // RING, k)

        block = scope.enter_context(nc.Block())

        @block.sync
        def _(sp):
            sp.dma_start(gates_in[:, 0:1], g_xattn.rearrange("(a n) -> a n", a=1).to_broadcast([P, 1])).then_inc(consts_loaded, 16)
            sp.dma_start(gates_in[:, 1:2], g_ffn.rearrange("(a n) -> a n", a=1).to_broadcast([P, 1])).then_inc(consts_loaded, 16)

            def load(r, k):
                b = RING * r + k
                wait(sp, av_done, b - RING + 1)
                wait(sp, x1_done, b - RING + 1)
                sp.dma_start(x_in[:, k], x[bass.ds(b, 1)].rearrange("b s d -> (b s) d")).then_inc(in_loaded[k], 16)
                sp.dma_start(ctx_in[:, k], ctx[bass.ds(b, 1)].rearrange("b s d -> (b s) d")).then_inc(in_loaded[k], 16)
                if isinstance(b, int) and b == 0:
                    sp.dma_start(mask_in[:, :], mask.rearrange("b m -> (b m)").rearrange("(a n) -> a n", a=1).to_broadcast([P, B * M])).then_inc(consts_loaded, 16)

            def store(r, k):
                b = RING * r + k
                t = k % TILES
                sp.wait_ge(nT_copied, b + 1)
                sp.dma_start(xnT_dram[bass.ds(2 * r + k // TILES, 1), :, :, t * P:(t + 1) * P].rearrange("r p c n -> (r p) c n"),
                             x1nT[:, t]).then_inc(xnT_stored[t], 16)

            for k in range(RING):
                load(0, k)
                if k == 3:
                    sp.dma_start(gu_raw[:, 0], gate_view[:, :, 0:IQ]).then_inc(gate_raw_loaded, 16)
                if k == 5:
                    sp.dma_start(gu_raw[:, 1], up_view[:, :, 0:IQ]).then_inc(up_raw_loaded, 16)
            with sp.Fori(1, B // RING) as r:
                for k in range(RING):
                    load(r, k)
                    store(r - 1, k)
            sp.wait_ge(gu_lo_done, 2 * GROUP)
            sp.dma_start(dn_raw.rearrange("p c n -> p (c n)"), down_view[0]).then_inc(dn_raw_loaded, 16)
            for k in range(RING):
                store(B // RING - 1, k)
            for t in range(TILES):
                sp.wait_ge(xnT_stored[t], 16 * (B // TILES))

        @block.gpsimd
        def _(pool):
            nc.gpsimd.memset(minus_half[:], -0.5).then_inc(half_done, 1)
            nc.gpsimd.memset(ident[:], 0.0).then_inc(ident_set, 1)
            pool.wait_ge(ident_set, 1)
            nc.gpsimd.affine_select(out=ident[:], in_=ident[:], compare_op=ALU.not_equal, fill=1.0, base=0,
                                    pattern=[[-1, P]], channel_multiplier=1).then_inc(ident_done, 1)
            pool.wait_ge(half_done, 1)

            pool.wait_ge(consts_loaded, 48)
            nc.gpsimd.tensor_scalar(mask_neg[:], mask_in[:], -BIG, BIG, ALU.mult, ALU.add).then_inc(mask_neg_done, 1)

            def slot(at, it, k0):
                if at(0) is not None:
                    r, k = at(0)
                    b = RING * r + k
                    wait(pool, xT_done, b - 1)
                    pool.wait_ge(var_eps_done[0], b + 1)
                    nc.gpsimd.tensor_tensor(rstd[:, 0, k:k + 1], var_eps[:, 0, k:k + 1], minus_half[:],
                                            ALU.pow).then_inc(rstd_done[0], 1)
                    wait_apart(pool, rstd_done[0], b + 1, half_done)
                    nc.gpsimd.tensor_scalar(xn[:, k % 2], x_in[:, k], bn_mv[:, 0, k, 0:1],
                                            rstd[:, 0, k:k + 1], ALU.subtract, ALU.mult).then_inc(xn_done, 1)
                if at(6) is not None:
                    r, k = at(6)
                    pool.wait_ge(var_eps_done[1], RING * r + k + 1)
                    nc.gpsimd.tensor_tensor(rstd[:, 1, k:k + 1], var_eps[:, 1, k:k + 1], minus_half[:],
                                            ALU.pow).then_inc(rstd_done[1], 1)

            slots(pool, slot)

        @block.scalar
        def _(act):
            act.wait_ge(consts_loaded, 48)
            nc.scalar.activation(xattn_gate[:], gates_in[:, 0:1], ACT.Tanh).then_inc(gates_done, 1)
            nc.scalar.activation(ffn_gate[:], gates_in[:, 1:2], ACT.Tanh).then_inc(gates_done, 1)

            def slot(at, it, k0):
                if at(1) is not None:
                    r, k = at(1)
                    b = RING * r + k
                    wait(act, scores_done, b - 1)
                    act.wait_ge(xT_done, b + 1)
                    nc.scalar.activation(xnT[:, k % 2], ps_xT[:], ACT.Copy).then_inc(xT_copied, 1)
                    act.wait_ge(cT_done, b + 1)
                    nc.scalar.activation(ctxT[:, k % 2], ps_cT[:], ACT.Copy).then_inc(cT_copied, 1)
                if at(3) is not None:
                    r, k = at(3)
                    b = RING * r + k
                    act.wait_ge(neg_max_done, b + 1)
                    wait(act, pT_done, b - 1)
                    nc.scalar.activation(probs[:, k % 2], neg_scores[:, k % 2], ACT.Exp, bias=neg_max[:, k:k + 1],
                                         scale=-1.0, accum_out=prob_sum[:, k:k + 1]).then_inc(probs_done, 1)
                if at(4) is not None:
                    r, k = at(4)
                    b = RING * r + k
                    act.wait_ge(pT_done, b + 1)
                    wait(act, av_done, b - 1)
                    nc.scalar.activation(probsT[:, k % 2], ps_pT[:, 0:P], ACT.Copy).then_inc(pT_copied, 1)
                if at(7) is not None:
                    r, k = at(7)
                    b = RING * r + k
                    t = k % TILES
                    wait(act, xnT_stored[t], 16 * (2 * r + k // TILES))
                    act.wait_ge(nT_done, b + 1)
                    nc.scalar.activation(x1nT[:, t], ps_nT[:], ACT.Copy).then_inc(nT_copied, 1)
                if it == 0 and k0 >= GROUP:
                    split_gu_hi(act, 0, k0 - GROUP)
                if it == B // RING and k0 < GROUP:
                    split_dn_hi(act, 0, k0)

            slots(act, slot)

        @block.vector
        def _(dve):
            def slot(at, it, k0):
                if at(0) is not None:
                    r, k = at(0)
                    b = RING * r + k
                    dve.wait_ge(in_loaded[k], 32 * (r + 1))
                    nc.vector.bn_stats(bn6[:, 0, k % 2], x_in[:, k]).then_inc(bn1_done, 1)
                if at(3) is not None:
                    r, k = at(3)
                    b = RING * r + k
                    wait(dve, probs_done, b - 1)
                    dve.wait_ge(scores_done, b + 1)
                    if isinstance(b, int) and b == 0:
                        dve.wait_ge(mask_neg_done, 1)
                    nc.vector.scalar_tensor_tensor(neg_scores[:, k % 2], ps_sc[k % 2][:, 0:M], -SCALE,
                                                   mask_neg[:, bass.ds(b * M, M)], ALU.mult, ALU.add).then_inc(neg_scores_done, 1)
                if at(0) is not None:
                    r, k = at(0)
                    b = RING * r + k
                    wait_apart(dve, bn1_done, b + 1, bn1_done)
                    nc.vector.bn_aggr(bn_mv[:, 0, k], bn6[:, 0, k % 2]).then_inc(stats1_done, 1)
                    dve.wait_ge(stats1_done, b + 1)
                    nc.vector.tensor_scalar(var_eps[:, 0, k:k + 1], bn_mv[:, 0, k, 1:2], EPS, None,
                                            ALU.add).then_inc(var_eps_done[0], 1)
                if at(6) is not None:
                    r, k = at(6)
                    b = RING * r + k
                    dve.wait_ge(probs_done, b + 1)
                    nc.vector.reciprocal(out_scale[:, k:k + 1], prob_sum[:, k:k + 1]).then_inc(scale_step, 1)
                if at(3) is not None:
                    r, k = at(3)
                    b = RING * r + k
                    dve.wait_ge(neg_scores_done, b + 1)
                    nc.vector.tensor_reduce(neg_max[:, k:k + 1], neg_scores[:, k % 2], AX.X, ALU.min).then_inc(neg_max_done, 1)
                if at(6) is not None:
                    r, k = at(6)
                    b = RING * r + k
                    dve.wait_ge(scale_step, 2 * b + 1)
                    if isinstance(b, int) and b == 0:
                        dve.wait_ge(gate_valid_done, 1)
                    nc.vector.tensor_tensor(out_scale[:, k:k + 1], out_scale[:, k:k + 1], gate_valid[:, bass.ds(b, 1)],
                                            ALU.mult).then_inc(scale_step, 1)
                    dve.wait_ge(scale_step, 2 * b + 2)
                    dve.wait_ge(av_done, b + 1)
                    row = rows[:, bass.ds(b * D, D)]
                    nc.vector.scalar_tensor_tensor(row, ps_av[k % 2][:], out_scale[:, k:k + 1], x_in[:, k],
                                                   ALU.mult, ALU.add).then_inc(x1_done, 1)
                    wait_apart(dve, x1_done, b + 1, bn1_done)
                    nc.vector.bn_stats(bn6[:, 1, k % 2], row).then_inc(bn2_done, 1)
                    wait_apart(dve, bn2_done, b + 1, bn1_done)
                    nc.vector.bn_aggr(bn_mv[:, 1, k], bn6[:, 1, k % 2]).then_inc(stats2_done, 1)
                    dve.wait_ge(stats2_done, b + 1)
                    nc.vector.tensor_scalar(var_eps[:, 1, k:k + 1], bn_mv[:, 1, k, 1:2], EPS, None,
                                            ALU.add).then_inc(var_eps_done[1], 1)
                if at(7) is not None:
                    r, k = at(7)
                    b = RING * r + k
                    wait(dve, nT_done, b - 1)
                    dve.wait_ge(rstd_done[1], b + 1)
                    nc.vector.tensor_scalar(x1n[:, k % 2], rows[:, bass.ds(b * D, D)], bn_mv[:, 1, k, 0:1],
                                            rstd[:, 1, k:k + 1], ALU.subtract, ALU.mult).then_inc(x1n_done, 1)
                if it == 0 and k0 == 3:
                    dve.wait_ge(consts_loaded, 48)
                    nc.vector.tensor_reduce(valid[:], mask_in[:].rearrange("p (b m) -> p b m", m=M), AX.X,
                                            ALU.max).then_inc(valid_done, 1)
                    dve.wait_ge(valid_done, 1)
                    dve.wait_ge(gates_done, 1)
                    nc.vector.tensor_scalar(gate_valid[:], valid[:], xattn_gate[:], None, ALU.mult).then_inc(gate_valid_done, 1)
                if it == 0 and k0 >= GROUP:
                    split_gu_lo(dve, 0, k0 - GROUP)
                if it == B // RING and k0 < GROUP:
                    split_dn_lo(dve, 0, k0)

            slots(dve, slot)

        @block.tensor
        def _(pe):
            pe.wait_ge(ident_done, 1)

            def slot(at, it, k0):
                if at(1) is not None:
                    r, k = at(1)
                    b = RING * r + k
                    pe.wait_ge(xn_done, b + 1)
                    wait(pe, xT_copied, b)
                    for c in range(KC):
                        last = nc.tensor.transpose(ps_xT[:, c], xn[:, k % 2, c * P:(c + 1) * P], ident[:])
                    last.then_inc(xT_done, 1)
                    pe.wait_ge(in_loaded[k], 32 * (r + 1))
                    wait(pe, cT_copied, b)
                    for c in range(KC):
                        last = nc.tensor.transpose(ps_cT[:, c], ctx_in[:, k, c * P:(c + 1) * P], ident[:])
                    last.then_inc(cT_done, 1)
                if at(2) is not None:
                    r, k = at(2)
                    b = RING * r + k
                    pe.wait_ge(xT_copied, b + 1)
                    pe.wait_ge(cT_copied, b + 1)
                    wait(pe, neg_scores_done, b - 1)
                    for c in range(KC):
                        last = nc.tensor.matmul(ps_sc[k % 2][:, 0:M], xnT[:, k % 2, c], ctxT[:, k % 2, c],
                                                start=(c == 0), stop=(c == KC - 1))
                    last.then_inc(scores_done, 1)
                if at(4) is not None:
                    r, k = at(4)
                    b = RING * r + k
                    pe.wait_ge(probs_done, b + 1)
                    wait(pe, pT_copied, b)
                    nc.tensor.transpose(ps_pT[:, 0:P], probs[:, k % 2], ident[:]).then_inc(pT_done, 1)
                if at(5) is not None:
                    r, k = at(5)
                    b = RING * r + k
                    pe.wait_ge(pT_copied, b + 1)
                    wait(pe, x1_done, b - 1)
                    nc.tensor.matmul(ps_av[k % 2][:], probsT[:, k % 2], ctx_in[:, k], start=True,
                                     stop=True).then_inc(av_done, 1)
                if at(7) is not None:
                    r, k = at(7)
                    b = RING * r + k
                    pe.wait_ge(x1n_done, b + 1)
                    wait(pe, nT_copied, b)
                    for c in range(KC):
                        last = nc.tensor.transpose(ps_nT[:, c], x1n[:, k % 2, c * P:(c + 1) * P], ident[:])
                    last.then_inc(nT_done, 1)

            slots(pe, slot)


def feed_forward(nc, sb, sem, shared):
    rows, ffn_gate, gu_raw, dn_raw = (shared[n] for n in ("rows", "ffn_gate", "gu_raw", "dn_raw"))
    gu_hi, gu_lo, dn_hi, dn_lo = (shared[n] for n in ("gu_hi", "gu_lo", "dn_hi", "dn_lo"))
    xnT_dram, out_view = shared["xnT_dram"], shared["out_view"]
    gate_view, up_view, down_view = shared["gate_view"], shared["up_view"], shared["down_view"]
    gate_raw_loaded, up_raw_loaded, dn_raw_loaded = (shared[n] for n in ("gate_raw_loaded", "up_raw_loaded", "dn_raw_loaded"))
    gu_lo_done, dn_lo_done = shared["gu_lo_done"], shared["dn_lo_done"]
    split_gu_hi, split_gu_lo, split_dn_hi, split_dn_lo = (
        shared[n] for n in ("split_gu_hi", "split_gu_lo", "split_dn_hi", "split_dn_lo"))
    STEPS = PASSES * BLOCKS

    scope = ExitStack()
    with scope:
        def sbuf(name, shape, dtype=F32):
            return sb(name, shape, dtype, scope)

        def psum(name, shape):
            return scope.enter_context(nc.psum_tensor(name, shape, F32))

        def semaphore(name):
            return sem(name, scope)

        x_raw = sbuf("x_raw", [P, KC, ROWS])
        x_hi = sbuf("x_hi", [P, KC, ROWS], F32R)
        x_lo = sbuf("x_lo", [P, KC, ROWS], F32R)
        silu = sbuf("silu", [P, 2, ROWS])
        hidden = sbuf("hidden", [P, GROUP, ROWS])
        hidden_abs = sbuf("hidden_abs", [P, GROUP, ROWS])
        beats = sbuf("beats", [P, 6, ROWS], BF16)
        part = sbuf("part", [P, 4, ROWS], BF16)
        wins = sbuf("wins", [P, 4, ROWS], BF16)
        h_hi = sbuf("h_hi", [P, GROUP, ROWS], F32R)
        h_lo = sbuf("h_lo", [P, GROUP, ROWS], F32R)

        ps_gate = [psum(f"ps_gate{i}", [P, ROWS]) for i in range(2)]
        ps_up = [psum(f"ps_up{i}", [P, ROWS]) for i in range(2)]
        ps_y = [psum(f"ps_y{i}", [P, D]) for i in range(TILES)]

        x_loaded, x_hi_done, x_lo_done = semaphore("x_loaded"), semaphore("x_hi_done"), semaphore("x_lo_done")
        gate_done, up_done, silu_done = semaphore("gate_done"), semaphore("up_done"), semaphore("silu_done")
        hidden_done, abs_done, beats_done = semaphore("hidden_done"), semaphore("abs_done"), semaphore("beats_done")
        part_done, wins_done, kept_done = semaphore("part_done"), semaphore("wins_done"), semaphore("kept_done")
        h_hi_done, h_lo_done = semaphore("h_hi_done"), semaphore("h_lo_done")
        y_done, y_added, stored = semaphore("y_done"), semaphore("y_added"), semaphore("stored")

        def steps(engine, step):
            step(0, 0, 0)
            with engine.Fori(0, PASSES - 1) as q:
                with engine.Fori(1, BLOCKS - 1) as r:
                    step(q * BLOCKS + r, q, r)
                step(q * BLOCKS + BLOCKS - 1, q, BLOCKS - 1, last=True)
                step(q * BLOCKS + BLOCKS, q + 1, 0, first=True)
            q = PASSES - 1
            with engine.Fori(1, BLOCKS - 1) as r:
                step(q * BLOCKS + r, q, r, final=True)
            step(q * BLOCKS + BLOCKS - 1, q, BLOCKS - 1, final=True)

        block = scope.enter_context(nc.Block())

        @block.sync
        def _(sp):
            def load_x(s, r):
                wait(sp, x_hi_done, KC * s)
                wait(sp, x_lo_done, KC * s)
                sp.dma_start(x_raw[:].rearrange("p c n -> p (c n)"),
                             xnT_dram[bass.ds(r, 1)].rearrange("r p c n -> (r p) (c n)")).then_inc(x_loaded, 16)

            def load_gu_raw(q):
                sp.wait_ge(dn_lo_done, GROUP * q)
                sp.dma_start(gu_raw[:, 0], gate_view[:, :, bass.ds(q * IQ, IQ)]).then_inc(gate_raw_loaded, 16)
                sp.dma_start(gu_raw[:, 1], up_view[:, :, bass.ds(q * IQ, IQ)]).then_inc(up_raw_loaded, 16)

            def store_block(s, r):
                sp.wait_ge(y_added, TILES * (s + 1))
                sp.dma_start(out_view[:, bass.ds(r * TILES, TILES), :],
                             rows[:, bass.ds(r * TILES * D, TILES * D)].rearrange("p (b d) -> p b d", d=D)
                             ).then_inc(stored, 16)

            load_x(0, 0)
            with sp.Fori(0, PASSES - 1) as q:
                load_x(q * BLOCKS + 1, 1)
                load_gu_raw(q + 1)
                with sp.Fori(2, BLOCKS) as r:
                    load_x(q * BLOCKS + r, r)
                load_x(q * BLOCKS + BLOCKS, 0)
                sp.wait_ge(gu_lo_done, 2 * GROUP * (q + 2))
                sp.dma_start(dn_raw.rearrange("p c n -> p (c n)"),
                             down_view[bass.ds(q + 1, 1)].rearrange("q p n -> (q p) n")).then_inc(dn_raw_loaded, 16)
            base = (PASSES - 1) * BLOCKS
            load_x(base + 1, 1)
            with sp.Fori(2, BLOCKS) as r:
                load_x(base + r, r)
                store_block(base + r - 2, r - 2)
            store_block(STEPS - 2, BLOCKS - 2)
            store_block(STEPS - 1, BLOCKS - 1)
            sp.wait_ge(stored, 16 * BLOCKS)

        def split_x_hi(act, s):
            act.wait_ge(x_loaded, 16 * (s + 1))
            wait(act, up_done, GROUP * s)
            for c in range(KC):
                nc.scalar.activation(x_hi[:, c], x_raw[:, c], ACT.Copy).then_inc(x_hi_done, 1)

        def split_x_lo(dve, s):
            for c in range(KC):
                dve.wait_ge(x_hi_done, KC * s + c + 1)
                nc.vector.tensor_tensor(x_lo[:, c], x_raw[:, c], x_hi[:, c].bitcast(F32),
                                        ALU.subtract).then_inc(x_lo_done, 1)

        @block.scalar
        def _(act):
            def step(s, q, r, first=False, last=False, final=False):
                for j in range(GROUP):
                    n = GROUP * s + j
                    act.wait_ge(gate_done, n + 1)
                    wait(act, hidden_done, n - 1)
                    nc.scalar.activation(silu[:, j % 2], ps_gate[j % 2][:], ACT.Silu).then_inc(silu_done, 1)
                    act.wait_ge(hidden_done, n + 1)
                    nc.scalar.activation(hidden_abs[:, j], hidden[:, j], ACT.Abs).then_inc(abs_done, 1)
                    if last:
                        split_gu_hi(act, q + 1, j)
                if not (final and isinstance(r, int)):
                    split_x_hi(act, s + 1)
                wait(act, y_done, TILES * s)
                for j in range(GROUP):
                    act.wait_ge(kept_done, GROUP * s + j + 1)
                    nc.scalar.activation(h_hi[:, j], hidden[:, j], ACT.Copy).then_inc(h_hi_done, 1)
                if first:
                    for j in range(GROUP):
                        split_dn_hi(act, q, j)

            split_x_hi(act, 0)
            steps(act, step)

        @block.vector
        def _(dve):
            def compare(s, i, j):
                dve.wait_ge(abs_done, GROUP * s + j + 1)
                return nc.vector.tensor_tensor(beats[:, PAIR[i, j]], hidden_abs[:, i], hidden_abs[:, j], ALU.is_ge)

            def add_y(s, r):
                for t in range(TILES):
                    dve.wait_ge(y_done, TILES * s + t + 1)
                    row = rows[:, bass.ds((TILES * r + t) * D, D)]
                    nc.vector.scalar_tensor_tensor(row, ps_y[t][:], ffn_gate[:], row, ALU.mult,
                                                   ALU.add).then_inc(y_added, 1)

            def step(s, q, r, first=False, last=False, final=False):
                for j in range(GROUP):
                    n = GROUP * s + j
                    wait(dve, h_lo_done, n - GROUP + 1)
                    dve.wait_ge(silu_done, n + 1)
                    dve.wait_ge(up_done, n + 1)
                    nc.vector.tensor_tensor(hidden[:, j], ps_up[j % 2][:], silu[:, j % 2], ALU.mult).then_inc(hidden_done, 1)
                    for i in range(j - 1):
                        compare(s, i, j - 1)
                    if last:
                        split_gu_lo(dve, q + 1, j)
                if not (final and isinstance(r, int)):
                    split_x_lo(dve, s + 1)
                for i in range(GROUP - 1):
                    compared = compare(s, i, GROUP - 1)
                compared.then_inc(beats_done, 1)
                dve.wait_ge(beats_done, s + 1)
                nc.vector.tensor_tensor(part[:, 0:2], beats[:, 2:4], beats[:, 0:2], ALU.subtract)
                nc.vector.tensor_tensor(part[:, 2], beats[:, PAIR[0, 1]], beats[:, PAIR[0, 2]], ALU.add)
                nc.vector.tensor_tensor(part[:, 3], beats[:, PAIR[1, 3]], beats[:, PAIR[2, 3]], ALU.add).then_inc(part_done, 1)
                dve.wait_ge(part_done, s + 1)
                nc.vector.tensor_tensor(wins[:, 0:2], part[:, 0:2],
                                        beats[:, PAIR[1, 2]:PAIR[1, 2] + 1].to_broadcast([P, 2, ROWS]), ALU.add)
                nc.vector.tensor_tensor(wins[:, 2:4], part[:, 2:4],
                                        beats[:, PAIR[0, 3]:PAIR[0, 3] + 1].to_broadcast([P, 2, ROWS]),
                                        ALU.add).then_inc(wins_done, 1)
                dve.wait_ge(wins_done, s + 1)
                for j in range(GROUP):
                    at, test, bound = KEEP[j]
                    nc.vector.scalar_tensor_tensor(hidden[:, j], wins[:, at], bound, hidden[:, j], test,
                                                   ALU.mult).then_inc(kept_done, 1)
                if first:
                    add_y(s - 1, BLOCKS - 1)
                elif not isinstance(s, int) or s > 0:
                    add_y(s - 1, r - 1)
                for j in range(GROUP):
                    dve.wait_ge(h_hi_done, GROUP * s + j + 1)
                    nc.vector.tensor_tensor(h_lo[:, j], hidden[:, j], h_hi[:, j].bitcast(F32),
                                            ALU.subtract).then_inc(h_lo_done, 1)
                if first:
                    for j in range(GROUP):
                        split_dn_lo(dve, q, j)

            split_x_lo(dve, 0)
            steps(dve, step)
            add_y(STEPS - 1, BLOCKS - 1)

        @block.tensor
        def _(pe):
            def three_products(bank, a_hi, a_lo, b_hi, b_lo, start, stop):
                nc.tensor.matmul(bank, a_hi, b_hi, start=start, stop=False)
                nc.tensor.matmul(bank, a_hi, b_lo, start=False, stop=False)
                return nc.tensor.matmul(bank, a_lo, b_hi, start=False, stop=stop)

            def gate_up(s, q=None):
                pe.wait_ge(x_hi_done, KC * (s + 1))
                pe.wait_ge(x_lo_done, KC * (s + 1))
                for j in range(GROUP):
                    n = GROUP * s + j
                    if q is not None:
                        pe.wait_ge(gu_lo_done, 2 * GROUP * q + 2 * j + 2)
                    wait(pe, silu_done, n - 1)
                    for c in range(KC):
                        last = three_products(ps_gate[j % 2][:], gu_hi[:, 0, j, c], gu_lo[:, 0, j, c],
                                              x_hi[:, c], x_lo[:, c], c == 0, c == KC - 1)
                    last.then_inc(gate_done, 1)
                    wait(pe, hidden_done, n - 1)
                    for c in range(KC):
                        last = three_products(ps_up[j % 2][:], gu_hi[:, 1, j, c], gu_lo[:, 1, j, c],
                                              x_hi[:, c], x_lo[:, c], c == 0, c == KC - 1)
                    last.then_inc(up_done, 1)

            def down(s, q=None):
                pe.wait_ge(h_lo_done, GROUP * (s + 1))
                if q is not None:
                    pe.wait_ge(dn_lo_done, GROUP * (q + 1))
                for t in range(TILES):
                    for j in range(GROUP):
                        at = slice(t * P, (t + 1) * P)
                        last = three_products(ps_y[t][:], h_hi[:, j, at], h_lo[:, j, at], dn_hi[:, j], dn_lo[:, j],
                                              j == 0, j == GROUP - 1)
                    last.then_inc(y_done, 1)

            def step(s, q, r, first=False, last=False, final=False):
                if isinstance(s, int) and s == 0:
                    gate_up(0, 0)
                    return
                gate_up(s, q if first else None)
                if not first:
                    down(s - 1, q if not isinstance(r, int) or r == 1 else None)
                else:
                    down(s - 1)

            steps(pe, step)
            down(STEPS - 1)


INS = ["x", "ctx_2048", "mask_BxS2_bk0", "g_xattn", "g_ffn", "L0_ffn_w_gate", "L0_ffn_w_up", "L0_ffn_w_down"]


def kernel(**inputs):
    import numpy as np
    import concourse.bacc as bacc
    from concourse.bass_utils import run_bass_kernel_spmd as run

    nc = bacc.Bacc("TRN2", target_bir_lowering=False, num_devices=1)
    arrays, args = {}, []
    for name in INS:
        a = np.ascontiguousarray(inputs[name])
        arrays[f"in_{name}"] = a
        args.append(nc.dram_tensor(f"in_{name}", a.shape, mybir.dt.from_np(a.dtype), kind="ExternalInput").ap())
    args.append(nc.dram_tensor("out_rows", (B, S, D), F32, kind="ExternalOutput").ap())
    flamingo_gated(nc, *args)
    r = run(nc, [arrays], core_ids=[0])
    return r.results[0]["out_rows"]
```

```python
from contextlib import ExitStack

import concourse.bass as bass
from concourse import mybir

F32 = mybir.dt.float32
F32R = mybir.dt.float32r
BF16 = mybir.dt.bfloat16
U8 = mybir.dt.uint8
ALU = mybir.AluOpType
ACT = mybir.ActivationFunctionType
AX = mybir.AxisListType

P = 128
B, S, D = 32, 128, 512
M = 128
I = 2048
KC = D // P
GROUP = 4
PASSES = I // (P * GROUP)
IQ = I // PASSES
ROWS = 512
TILES = ROWS // P
BLOCKS = B * S // ROWS
EPS = 1e-5
SCALE = float(D) ** -0.5
BIG = 1e30
RING = 8
LAST_LAG = 7
KEEP = {0: (2, ALU.is_ge, 2.0), 1: (0, ALU.is_ge, 1.0), 2: (1, ALU.is_le, 0.0), 3: (3, ALU.is_le, 1.0)}
PAIR = {(0, 1): 0, (2, 3): 1, (1, 3): 2, (0, 2): 3, (1, 2): 4, (0, 3): 5}


def wait(engine, semaphore, value):
    if not isinstance(value, int) or value > 0:
        engine.wait_ge(semaphore, value)


def wait_apart(engine, semaphore, value, started):
    if isinstance(value, int):
        wait(engine, semaphore, value)
        return
    engine.compute_val(value)
    engine.wait_ge(started, 1)
    engine.wait_ge(semaphore, value)


def flamingo_gated(nc, x, ctx, mask, g_xattn, g_ffn, w_gate, w_up, w_down, out):
    xnT_dram = nc.dram_tensor("xnT_scratch", [BLOCKS, P, KC, ROWS], F32).ap()
    gate_view = w_gate.rearrange("(c p) i -> p c i", p=P)
    up_view = w_up.rearrange("(c p) i -> p c i", p=P)
    down_view = w_down.rearrange("(q p j) n -> q p (j n)", p=P, j=GROUP)
    out_view = out.rearrange("b s d -> s b d")

    whole = ExitStack()
    with whole:
        def sb(name, shape, dtype, scope=whole):
            return scope.enter_context(nc.sbuf_tensor(name, shape, dtype))

        def sem(name, scope=whole):
            return scope.enter_context(nc.semaphore(name))

        rows = sb("rows", [P, B * D], F32)
        gu_hi = sb("gu_hi", [P, 2, GROUP, KC, P], F32R)
        gu_lo = sb("gu_lo", [P, 2, GROUP, KC, P], F32R)
        dn_hi = sb("dn_hi", [P, GROUP, D], F32R)
        dn_lo = sb("dn_lo", [P, GROUP, D], F32R)
        gu_raw = sb("gu_raw", [P, 2, KC, IQ], F32)
        dn_raw = gu_raw[:, 0]
        x_raw = sb("x_raw", [P, KC, ROWS], F32)
        ffn_gate = sb("ffn_gate", [P, 1], F32)

        x_loaded, x_hi_done, x_lo_done = sem("x_loaded"), sem("x_hi_done"), sem("x_lo_done")
        xnT_stored = [sem(f"xnT_stored{k}") for k in range(TILES)]
        gate_raw_loaded, up_raw_loaded, dn_raw_loaded = sem("gate_raw_loaded"), sem("up_raw_loaded"), sem("dn_raw_loaded")
        gu_hi_done, gu_lo_done = sem("gu_hi_done"), sem("gu_lo_done")
        dn_hi_done, dn_lo_done = sem("dn_hi_done"), sem("dn_lo_done")

        def gu_raw_of(g, j):
            return gu_raw[:, g, :, j:IQ:GROUP]

        def split_gu_hi(act, q, j):
            act.wait_ge(gate_raw_loaded, 16 * (q + 1))
            act.wait_ge(up_raw_loaded, 16 * (q + 1))
            for g in range(2):
                nc.scalar.activation(gu_hi[:, g, j], gu_raw_of(g, j), ACT.Copy).then_inc(gu_hi_done, 1)

        def split_gu_lo(engine, instructions, q, j, which=range(2)):
            for g in which:
                engine.wait_ge(gu_hi_done, 2 * GROUP * q + 2 * j + g + 1)
                instructions.tensor_tensor(gu_lo[:, g, j], gu_raw_of(g, j), gu_hi[:, g, j].bitcast(F32),
                                        ALU.subtract).then_inc(gu_lo_done, 1)

        def split_dn_hi(act, q, j):
            act.wait_ge(dn_raw_loaded, 16 * (q + 1))
            nc.scalar.activation(dn_hi[:, j], dn_raw[:, j], ACT.Copy).then_inc(dn_hi_done, 1)

        def split_dn_lo(engine, instructions, q, j):
            engine.wait_ge(dn_hi_done, GROUP * q + j + 1)
            instructions.tensor_tensor(dn_lo[:, j], dn_raw[:, j], dn_hi[:, j].bitcast(F32),
                                    ALU.subtract).then_inc(dn_lo_done, 1)

        def split_first_x_hi(act, c):
            act.wait_ge(x_loaded, 16)
            nc.scalar.activation(dn_hi[:, c], x_raw[:, c], ACT.Copy).then_inc(x_hi_done, 1)

        def split_first_x_lo(dve, c):
            dve.wait_ge(x_hi_done, c + 1)
            nc.vector.tensor_tensor(dn_lo[:, c], x_raw[:, c], dn_hi[:, c].bitcast(F32),
                                    ALU.subtract).then_inc(x_lo_done, 1)

        attention(nc, sb, sem, locals())
        feed_forward(nc, sb, sem, locals())


def attention(nc, sb, sem, shared):
    x, ctx, mask, g_xattn, g_ffn = (shared[n] for n in ("x", "ctx", "mask", "g_xattn", "g_ffn"))
    rows, gu_raw, dn_raw, ffn_gate = (shared[n] for n in ("rows", "gu_raw", "dn_raw", "ffn_gate"))
    xnT_dram, x_raw, x_loaded, xnT_stored = (shared[n] for n in ("xnT_dram", "x_raw", "x_loaded", "xnT_stored"))
    gate_view, up_view, down_view = shared["gate_view"], shared["up_view"], shared["down_view"]
    gate_raw_loaded, up_raw_loaded, dn_raw_loaded = (shared[n] for n in ("gate_raw_loaded", "up_raw_loaded", "dn_raw_loaded"))
    gu_lo_done = shared["gu_lo_done"]
    split_gu_hi, split_gu_lo = shared["split_gu_hi"], shared["split_gu_lo"]
    split_first_x_hi, split_first_x_lo = shared["split_first_x_hi"], shared["split_first_x_lo"]

    scope = ExitStack()
    with scope:
        def sbuf(name, shape, dtype=F32):
            return sb(name, shape, dtype, scope)

        def psum(name, shape):
            return scope.enter_context(nc.psum_tensor(name, shape, F32))

        def semaphore(name):
            return sem(name, scope)

        x1nT = sbuf("x1nT", [P, TILES, KC, P])
        x_in = sbuf("x_in", [P, RING, D])
        ctx_in = sbuf("ctx_in", [P, RING, D])
        xn = sbuf("xn", [P, 2, D])
        xnT = sbuf("xnT", [P, 2, KC, P])
        ctxT = sbuf("ctxT", [P, 2, KC, P])
        mask_in = x1nT[:, 0:B * M // (4 * D)].rearrange("p t c n -> p (t c n)").bitcast(U8)
        mask_neg = sbuf("mask_neg", [P, B * M], BF16)
        neg_scores = sbuf("neg_scores", [P, 2, M])
        neg_max = sbuf("neg_max", [P, RING])
        probs = sbuf("probs", [P, 2, M])
        probsT = sbuf("probsT", [P, 2, P])
        prob_sum = sbuf("prob_sum", [P, RING])
        inv_sum = sbuf("inv_sum", [P, RING])
        out_scale = sbuf("out_scale", [P, RING])
        x1n = sbuf("x1n", [P, 2, D])
        bn6 = sbuf("bn6", [P, 2, 2, 6])
        bn_mv = sbuf("bn_mv", [P, 2, RING, 2])
        var_eps = sbuf("var_eps", [P, 2, RING])
        neg_mean = sbuf("neg_mean", [P, RING])
        neg_mean_rstd = sbuf("neg_mean_rstd", [P, RING])
        eps = sbuf("eps", [P, 1])
        minus_one = sbuf("minus_one", [P, 1])
        rstd = sbuf("rstd", [P, 2, RING])
        minus_half = sbuf("minus_half", [P, 1])
        xattn_gate = sbuf("xattn_gate", [P, 1])
        gates_in = sbuf("gates_in", [P, 2])
        valid = sbuf("valid", [P, B])
        gate_valid = sbuf("gate_valid", [P, B])
        ident = sbuf("ident", [P, P])

        ps_xT = psum("ps_xT", [P, KC, P])
        ps_cT = psum("ps_cT", [P, KC, P])
        ps_sc = [psum(f"ps_sc{i}", [P, 512]) for i in range(2)]
        ps_pT = psum("ps_pT", [P, 512])
        ps_av = [psum(f"ps_av{i}", [P, D]) for i in range(2)]
        ps_nT = psum("ps_nT", [P, KC, P])

        in_loaded = [semaphore(f"in_loaded{k}") for k in range(RING)]
        gates_loaded, mask_loaded = semaphore("gates_loaded"), semaphore("mask_loaded")
        neg_mean_done, shift_done = semaphore("neg_mean_done"), semaphore("shift_done")
        ident_set, ident_done, half_done = semaphore("ident_set"), semaphore("ident_done"), semaphore("half_done")
        gates_done, valid_done, gate_valid_done = semaphore("gates_done"), semaphore("valid_done"), semaphore("gate_valid_done")
        bn1_done, stats1_done = semaphore("bn1_done"), semaphore("stats1_done")
        bn2_done, stats2_done = semaphore("bn2_done"), semaphore("stats2_done")
        var_eps_done = [semaphore(f"var_eps{i}_done") for i in (1, 2)]
        rstd_done = [semaphore(f"rstd{i}_done") for i in (1, 2)]
        mask_neg_done, xn_done, x1n_done = semaphore("mask_neg_done"), semaphore("xn_done"), semaphore("x1n_done")
        xT_done, cT_done, xT_copied, cT_copied = (semaphore(n) for n in ("xT_done", "cT_done", "xT_copied", "cT_copied"))
        scores_done, neg_scores_done, neg_max_done = semaphore("scores_done"), semaphore("neg_scores_done"), semaphore("neg_max_done")
        probs_done, pT_done, pT_copied = semaphore("probs_done"), semaphore("pT_done"), semaphore("pT_copied")
        av_done, x1_done = semaphore("av_done"), semaphore("x1_done")
        inv_sum_done, out_scale_done = semaphore("inv_sum_done"), semaphore("out_scale_done")
        nT_done, nT_copied = semaphore("nT_done"), semaphore("nT_copied")

        def slots(engine, slot):
            def at_of(it, k):
                def at(lag):
                    r, kk = it + (k - lag) // RING, (k - lag) % RING
                    if isinstance(r, int) and not 0 <= r < B // RING:
                        return None
                    return r, kk
                return at
            for k in range(RING):
                slot(at_of(0, k), 0, k)
            with engine.Fori(1, B // RING) as it:
                for k in range(RING):
                    slot(at_of(it, k), None, k)
            for k in range(LAST_LAG):
                slot(at_of(B // RING, k), B // RING, k)

        block = scope.enter_context(nc.Block())

        @block.sync
        def _(sp):
            def load(r, k):
                b = RING * r + k
                wait(sp, av_done, b - RING + 1)
                wait(sp, x1_done, b - RING + 1)
                sp.dma_start(x_in[:, k], x[bass.ds(b, 1)].rearrange("b s d -> (b s) d")).then_inc(in_loaded[k], 16)
                sp.dma_start(ctx_in[:, k], ctx[bass.ds(b, 1)].rearrange("b s d -> (b s) d")).then_inc(in_loaded[k], 16)

            def store(r, k):
                b = RING * r + k
                t = k % TILES
                sp.wait_ge(nT_copied, b + 1)
                sp.dma_start(xnT_dram[bass.ds(2 * r + k // TILES, 1), :, :, t * P:(t + 1) * P].rearrange("r p c n -> (r p) c n"),
                             x1nT[:, t]).then_inc(xnT_stored[t], 16)

            for k in range(RING):
                load(0, k)
                if k == 0:
                    sp.dma_start(mask_in, mask.rearrange("b m -> (b m)").rearrange("(a n) -> a n", a=1)
                                 .to_broadcast([P, B * M])).then_inc(mask_loaded, 16)
                    for n, g in enumerate((g_xattn, g_ffn)):
                        sp.dma_start(gates_in[:, n:n + 1], g.rearrange("(a n) -> a n", a=1)
                                     .to_broadcast([P, 1])).then_inc(gates_loaded, 16)
            ahead = 2
            for k in range(ahead):
                load(1, k)
            sp.dma_start(gu_raw[:, 0], gate_view[:, :, 0:IQ]).then_inc(gate_raw_loaded, 16)
            sp.dma_start(gu_raw[:, 1], up_view[:, :, 0:IQ]).then_inc(up_raw_loaded, 16)
            with sp.Fori(1, B // RING - 1) as r:
                for k in range(RING):
                    store(r - 1, k)
                    load(r + (k + ahead) // RING, (k + ahead) % RING)
            for k in range(RING):
                store(B // RING - 2, k)
                if k + ahead < RING:
                    load(B // RING - 1, k + ahead)
            for t in range(TILES):
                sp.wait_ge(xnT_stored[t], 16)
            sp.dma_start(x_raw[:].rearrange("p c n -> p (c n)"),
                         xnT_dram[0].rearrange("p c n -> p (c n)")).then_inc(x_loaded, 16)
            for k in range(RING):
                store(B // RING - 1, k)

        @block.gpsimd
        def _(pool):
            nc.gpsimd.memset(eps[:], EPS)
            nc.gpsimd.memset(minus_one[:], -1.0)
            nc.gpsimd.memset(minus_half[:], -0.5).then_inc(half_done, 1)
            nc.gpsimd.memset(ident[:], 0.0).then_inc(ident_set, 1)
            pool.wait_ge(ident_set, 1)
            nc.gpsimd.affine_select(out=ident[:], in_=ident[:], compare_op=ALU.not_equal, fill=1.0, base=0,
                                    pattern=[[-1, P]], channel_multiplier=1).then_inc(ident_done, 1)
            pool.wait_ge(half_done, 1)

            def inverse_deviation(which, k, b):
                pool.wait_ge((stats1_done, stats2_done)[which], b + 1)
                nc.gpsimd.tensor_tensor(var_eps[:, which, k:k + 1], bn_mv[:, which, k, 1:2], eps[:],
                                        ALU.add).then_inc(var_eps_done[which], 1)
                if which == 0:
                    nc.gpsimd.tensor_tensor(neg_mean[:, k:k + 1], bn_mv[:, 0, k, 0:1], minus_one[:],
                                            ALU.mult).then_inc(neg_mean_done, 1)
                pool.wait_ge(var_eps_done[which], b + 1)
                nc.gpsimd.tensor_tensor(rstd[:, which, k:k + 1], var_eps[:, which, k:k + 1], minus_half[:],
                                        ALU.pow).then_inc(rstd_done[which], 1)

            def slot(at, it, k0):
                if at(6) is not None:
                    r, k = at(6)
                    inverse_deviation(1, k, RING * r + k)
                if at(0) is not None:
                    r, k = at(0)
                    b = RING * r + k
                    inverse_deviation(0, k, b)
                    pool.wait_ge(neg_mean_done, b + 1)
                    pool.wait_ge(rstd_done[0], b + 1)
                    nc.gpsimd.tensor_tensor(neg_mean_rstd[:, k:k + 1], neg_mean[:, k:k + 1], rstd[:, 0, k:k + 1],
                                            ALU.mult).then_inc(shift_done, 1)
                if at(4) is not None:
                    r, k = at(4)
                    b = RING * r + k
                    pool.wait_ge(probs_done, b + 1)
                    nc.gpsimd.tensor_tensor(inv_sum[:, k:k + 1], prob_sum[:, k:k + 1], minus_one[:],
                                            ALU.pow).then_inc(inv_sum_done, 1)
                    if isinstance(b, int) and b == 0:
                        pool.wait_ge(gate_valid_done, 1)
                    wait_apart(pool, inv_sum_done, b + 1, half_done)
                    nc.gpsimd.tensor_tensor(out_scale[:, k:k + 1], inv_sum[:, k:k + 1], gate_valid[:, bass.ds(b, 1)],
                                            ALU.mult).then_inc(out_scale_done, 1)
                if it == B // RING and k0 == 5:
                    split_gu_lo(pool, nc.gpsimd, 0, 0, [0])
                if it == 0 and k0 < 3:
                    pool.wait_ge(mask_loaded, 16)
                    for at_m in {0: (0,), 1: (1,), 2: (2, 3)}[k0]:
                        part = slice(at_m * RING * M, (at_m + 1) * RING * M)
                        nc.gpsimd.tensor_scalar(mask_neg[:, part], mask_in[:, part], -BIG, BIG, ALU.mult,
                                                ALU.add).then_inc(mask_neg_done, 1)

            slots(pool, slot)

        @block.scalar
        def _(act):
            def slot(at, it, k0):
                if at(1) is not None:
                    r, k = at(1)
                    b = RING * r + k
                    wait(act, scores_done, b - 1)
                    act.wait_ge(cT_done, b + 1)
                    nc.scalar.activation(ctxT[:, k % 2], ps_cT[:], ACT.Copy).then_inc(cT_copied, 1)
                    act.wait_ge(xT_done, b + 1)
                    nc.scalar.activation(xnT[:, k % 2], ps_xT[:], ACT.Copy).then_inc(xT_copied, 1)
                if at(3) is not None:
                    r, k = at(3)
                    b = RING * r + k
                    act.wait_ge(neg_max_done, b + 1)
                    wait(act, pT_done, b - 1)
                    nc.scalar.activation(probs[:, k % 2], neg_scores[:, k % 2], ACT.Exp, bias=neg_max[:, k:k + 1],
                                         scale=-1.0, accum_out=prob_sum[:, k:k + 1]).then_inc(probs_done, 1)
                if at(0) is not None:
                    r, k = at(0)
                    b = RING * r + k
                    wait(act, xT_done, b - 1)
                    act.wait_ge(shift_done, b + 1)
                    nc.scalar.activation(xn[:, k % 2], x_in[:, k], ACT.Identity, bias=neg_mean_rstd[:, k:k + 1],
                                         scale=rstd[:, 0, k:k + 1]).then_inc(xn_done, 1)
                if at(7) is not None:
                    r, k = at(7)
                    b = RING * r + k
                    t = k % TILES
                    wait(act, xnT_stored[t], 16 * (2 * r + k // TILES))
                    act.wait_ge(nT_done, b + 1)
                    nc.scalar.activation(x1nT[:, t], ps_nT[:], ACT.Copy).then_inc(nT_copied, 1)
                if at(3) is not None:
                    r, k = at(3)
                    b = RING * r + k
                    act.wait_ge(pT_done, b + 1)
                    wait(act, av_done, b - 1)
                    nc.scalar.activation(probsT[:, k % 2], ps_pT[:, 0:P], ACT.Copy).then_inc(pT_copied, 1)
                if it == 0 and k0 == 1:
                    act.wait_ge(gates_loaded, 32)
                    nc.scalar.activation(xattn_gate[:], gates_in[:, 0:1], ACT.Tanh).then_inc(gates_done, 1)
                    nc.scalar.activation(ffn_gate[:], gates_in[:, 1:2], ACT.Tanh).then_inc(gates_done, 1)
                if it == B // RING and k0 < GROUP:
                    split_gu_hi(act, 0, k0)
                if it == B // RING and 2 <= k0 < 2 + KC:
                    split_first_x_hi(act, k0 - 2)

            slots(act, slot)

        @block.vector
        def _(dve):
            def slot(at, it, k0):
                if at(0) is not None:
                    r, k = at(0)
                    b = RING * r + k
                    dve.wait_ge(in_loaded[k], 32 * (r + 1))
                    nc.vector.bn_stats(bn6[:, 0, k % 2], x_in[:, k]).then_inc(bn1_done, 1)
                if at(6) is not None:
                    r, k = at(6)
                    wait_apart(dve, bn2_done, RING * r + k + 1, bn1_done)
                    nc.vector.bn_aggr(bn_mv[:, 1, k], bn6[:, 1, k % 2]).then_inc(stats2_done, 1)
                if at(0) is not None:
                    r, k = at(0)
                    wait_apart(dve, bn1_done, RING * r + k + 1, bn1_done)
                    nc.vector.bn_aggr(bn_mv[:, 0, k], bn6[:, 0, k % 2]).then_inc(stats1_done, 1)
                if at(3) is not None:
                    r, k = at(3)
                    b = RING * r + k
                    wait(dve, probs_done, b - 1)
                    dve.wait_ge(scores_done, b + 1)
                    if isinstance(b, int) and b == 0:
                        dve.wait_ge(mask_neg_done, 4)
                    nc.vector.scalar_tensor_tensor(neg_scores[:, k % 2], ps_sc[k % 2][:, 0:M], -SCALE,
                                                   mask_neg[:, bass.ds(b * M, M)], ALU.mult, ALU.add).then_inc(neg_scores_done, 1)
                if at(3) is not None:
                    r, k = at(3)
                    dve.wait_ge(neg_scores_done, RING * r + k + 1)
                    nc.vector.tensor_reduce(neg_max[:, k:k + 1], neg_scores[:, k % 2], AX.X, ALU.min).then_inc(neg_max_done, 1)
                if at(5) is not None:
                    r, k = at(5)
                    b = RING * r + k
                    dve.wait_ge(out_scale_done, b + 1)
                    dve.wait_ge(av_done, b + 1)
                    nc.vector.scalar_tensor_tensor(rows[:, bass.ds(b * D, D)], ps_av[k % 2][:], out_scale[:, k:k + 1],
                                                   x_in[:, k], ALU.mult, ALU.add).then_inc(x1_done, 1)
                if at(6) is not None:
                    r, k = at(6)
                    b = RING * r + k
                    wait(dve, nT_done, b - 1)
                    dve.wait_ge(rstd_done[1], b + 1)
                    nc.vector.tensor_scalar(x1n[:, k % 2], rows[:, bass.ds(b * D, D)], bn_mv[:, 1, k, 0:1],
                                            rstd[:, 1, k:k + 1], ALU.subtract, ALU.mult).then_inc(x1n_done, 1)
                if at(5) is not None:
                    r, k = at(5)
                    b = RING * r + k
                    wait_apart(dve, x1_done, b + 1, bn1_done)
                    nc.vector.bn_stats(bn6[:, 1, k % 2], rows[:, bass.ds(b * D, D)]).then_inc(bn2_done, 1)
                if it == 0 and k0 == 3:
                    dve.wait_ge(mask_loaded, 16)
                    nc.vector.tensor_reduce(valid[:], mask_in.rearrange("p (b m) -> p b m", m=M), AX.X,
                                            ALU.max).then_inc(valid_done, 1)
                    dve.wait_ge(valid_done, 1)
                    dve.wait_ge(gates_done, 1)
                    nc.vector.tensor_scalar(gate_valid[:], valid[:], xattn_gate[:], None, ALU.mult).then_inc(gate_valid_done, 1)
            slots(dve, slot)
            for c in range(KC // 2):
                split_first_x_lo(dve, c)

        @block.tensor
        def _(pe):
            pe.wait_ge(ident_done, 1)

            def slot(at, it, k0):
                if at(1) is not None:
                    r, k = at(1)
                    b = RING * r + k
                    pe.wait_ge(in_loaded[k], 32 * (r + 1))
                    wait(pe, cT_copied, b)
                    for c in range(KC):
                        last = nc.tensor.transpose(ps_cT[:, c], ctx_in[:, k, c * P:(c + 1) * P], ident[:])
                    last.then_inc(cT_done, 1)
                    pe.wait_ge(xn_done, b + 1)
                    wait(pe, xT_copied, b)
                    for c in range(KC):
                        last = nc.tensor.transpose(ps_xT[:, c], xn[:, k % 2, c * P:(c + 1) * P], ident[:])
                    last.then_inc(xT_done, 1)
                if at(2) is not None:
                    r, k = at(2)
                    b = RING * r + k
                    pe.wait_ge(xT_copied, b + 1)
                    pe.wait_ge(cT_copied, b + 1)
                    wait(pe, neg_scores_done, b - 1)
                    for c in range(KC):
                        last = nc.tensor.matmul(ps_sc[k % 2][:, 0:M], xnT[:, k % 2, c], ctxT[:, k % 2, c],
                                                start=(c == 0), stop=(c == KC - 1))
                    last.then_inc(scores_done, 1)
                if at(7) is not None:
                    r, k = at(7)
                    b = RING * r + k
                    pe.wait_ge(x1n_done, b + 1)
                    wait(pe, nT_copied, b)
                    for c in range(KC):
                        last = nc.tensor.transpose(ps_nT[:, c], x1n[:, k % 2, c * P:(c + 1) * P], ident[:])
                    last.then_inc(nT_done, 1)
                if at(4) is not None:
                    r, k = at(4)
                    b = RING * r + k
                    pe.wait_ge(pT_copied, b + 1)
                    wait(pe, x1_done, b - 1)
                    nc.tensor.matmul(ps_av[k % 2][:], probsT[:, k % 2], ctx_in[:, k], start=True,
                                     stop=True).then_inc(av_done, 1)
                if at(3) is not None:
                    r, k = at(3)
                    b = RING * r + k
                    pe.wait_ge(probs_done, b + 1)
                    wait(pe, pT_copied, b)
                    nc.tensor.transpose(ps_pT[:, 0:P], probs[:, k % 2], ident[:]).then_inc(pT_done, 1)

            slots(pe, slot)


def feed_forward(nc, sb, sem, shared):
    rows, ffn_gate, gu_raw, dn_raw = (shared[n] for n in ("rows", "ffn_gate", "gu_raw", "dn_raw"))
    gu_hi, gu_lo, dn_hi, dn_lo = (shared[n] for n in ("gu_hi", "gu_lo", "dn_hi", "dn_lo"))
    xnT_dram, out_view, x_raw, xnT_stored = (shared[n] for n in ("xnT_dram", "out_view", "x_raw", "xnT_stored"))
    gate_view, up_view, down_view = shared["gate_view"], shared["up_view"], shared["down_view"]
    gate_raw_loaded, up_raw_loaded, dn_raw_loaded = (shared[n] for n in ("gate_raw_loaded", "up_raw_loaded", "dn_raw_loaded"))
    gu_lo_done, dn_lo_done = shared["gu_lo_done"], shared["dn_lo_done"]
    split_gu_hi, split_gu_lo, split_dn_hi, split_dn_lo = (
        shared[n] for n in ("split_gu_hi", "split_gu_lo", "split_dn_hi", "split_dn_lo"))
    split_first_x_lo = shared["split_first_x_lo"]
    STEPS = PASSES * BLOCKS

    scope = ExitStack()
    with scope:
        def sbuf(name, shape, dtype=F32):
            return sb(name, shape, dtype, scope)

        def psum(name, shape):
            return scope.enter_context(nc.psum_tensor(name, shape, F32))

        def semaphore(name):
            return sem(name, scope)

        h_lo = sbuf("h_lo", [P, GROUP, ROWS], F32R)
        x_hi = sbuf("x_hi", [P, KC, ROWS], F32R)
        x_lo = sbuf("x_lo", [P, KC, ROWS], F32R)
        silu = sbuf("silu", [P, 2, ROWS])
        hidden = sbuf("hidden", [P, GROUP, ROWS])
        hidden_abs = sbuf("hidden_abs", [P, GROUP, ROWS])
        beats = sbuf("beats", [P, 6, ROWS], BF16)
        part = sbuf("part", [P, 4, ROWS], BF16)
        wins = sbuf("wins", [P, 4, ROWS], BF16)
        h_hi = sbuf("h_hi", [P, GROUP, ROWS], F32R)

        ps_gate = [psum(f"ps_gate{i}", [P, ROWS]) for i in range(2)]
        ps_up = [psum(f"ps_up{i}", [P, ROWS]) for i in range(2)]
        ps_y = [psum(f"ps_y{i}", [P, D]) for i in range(TILES)]

        x_loaded, x_hi_done, x_lo_done = (shared[n] for n in ("x_loaded", "x_hi_done", "x_lo_done"))
        gate_done, up_done, silu_done = semaphore("gate_done"), semaphore("up_done"), semaphore("silu_done")
        hidden_done, abs_done, beats_done = semaphore("hidden_done"), semaphore("abs_done"), semaphore("beats_done")
        part_done, wins_done, kept_done = semaphore("part_done"), semaphore("wins_done"), semaphore("kept_done")
        h_hi_done, h_lo_done = semaphore("h_hi_done"), semaphore("h_lo_done")
        y_done, y_added, stored = semaphore("y_done"), semaphore("y_added"), semaphore("stored")

        def steps(engine, step):
            step(0, 0, 0, first=True)
            with engine.Fori(0, PASSES - 1) as q:
                with engine.Fori(1, BLOCKS - 1) as r:
                    step(q * BLOCKS + r, q, r)
                step(q * BLOCKS + BLOCKS - 1, q, BLOCKS - 1, last=True)
                step(q * BLOCKS + BLOCKS, q + 1, 0, first=True)
            q = PASSES - 1
            with engine.Fori(1, BLOCKS - 1) as r:
                step(q * BLOCKS + r, q, r)
            step(q * BLOCKS + BLOCKS - 1, q, BLOCKS - 1)

        block = scope.enter_context(nc.Block())

        @block.sync
        def _(sp):
            def load_x(s, r):
                wait(sp, x_hi_done, KC * s)
                wait(sp, x_lo_done, KC * s)
                sp.dma_start(x_raw[:].rearrange("p c n -> p (c n)"),
                             xnT_dram[bass.ds(r, 1)].rearrange("r p c n -> (r p) (c n)")).then_inc(x_loaded, 16)

            def load_gu_raw(q):
                sp.wait_ge(dn_lo_done, GROUP * q)
                sp.dma_start(gu_raw[:, 0], gate_view[:, :, bass.ds(q * IQ, IQ)]).then_inc(gate_raw_loaded, 16)
                sp.dma_start(gu_raw[:, 1], up_view[:, :, bass.ds(q * IQ, IQ)]).then_inc(up_raw_loaded, 16)

            def store_block(s, r):
                sp.wait_ge(y_added, TILES * (s + 1))
                sp.dma_start(out_view[:, bass.ds(r * TILES, TILES), :],
                             rows[:, bass.ds(r * TILES * D, TILES * D)].rearrange("p (b d) -> p b d", d=D)
                             ).then_inc(stored, 16)

            for t in range(TILES):
                sp.wait_ge(xnT_stored[t], 16 * BLOCKS)
            sp.wait_ge(gu_lo_done, 2 * GROUP)
            sp.dma_start(dn_raw.rearrange("p c n -> p (c n)"), down_view[0]).then_inc(dn_raw_loaded, 16)
            with sp.Fori(0, PASSES - 1) as q:
                load_x(q * BLOCKS + 1, 1)
                load_gu_raw(q + 1)
                with sp.Fori(2, BLOCKS) as r:
                    load_x(q * BLOCKS + r, r)
                load_x(q * BLOCKS + BLOCKS, 0)
                sp.wait_ge(gu_lo_done, 2 * GROUP * (q + 2))
                sp.dma_start(dn_raw.rearrange("p c n -> p (c n)"),
                             down_view[bass.ds(q + 1, 1)].rearrange("q p n -> (q p) n")).then_inc(dn_raw_loaded, 16)
            base = (PASSES - 1) * BLOCKS
            load_x(base + 1, 1)
            with sp.Fori(2, BLOCKS) as r:
                load_x(base + r, r)
                store_block(base + r - 2, r - 2)
            store_block(STEPS - 2, BLOCKS - 2)
            for t in range(TILES):
                sp.wait_ge(y_added, TILES * (STEPS - 1) + t + 1)
                at = (BLOCKS - 1) * TILES + t
                sp.dma_start(out_view[:, at], rows[:, at * D:(at + 1) * D]).then_inc(stored, 16)
            sp.wait_ge(stored, 16 * (BLOCKS - 1 + TILES))

        def split_x_hi(act, s):
            act.wait_ge(x_loaded, 16 * (s + 1))
            if not isinstance(s, int) or s > 1:
                wait(act, up_done, GROUP * s)
            for c in range(KC):
                nc.scalar.activation(x_hi[:, c], x_raw[:, c], ACT.Copy).then_inc(x_hi_done, 1)

        def split_x_lo(dve, s):
            for c in range(KC):
                dve.wait_ge(x_hi_done, KC * s + c + 1)
                nc.vector.tensor_tensor(x_lo[:, c], x_raw[:, c], x_hi[:, c].bitcast(F32),
                                        ALU.subtract).then_inc(x_lo_done, 1)

        @block.gpsimd
        def _(pool):
            split_gu_lo(pool, nc.gpsimd, 0, 0, [1])
            for j in range(1, GROUP):
                split_gu_lo(pool, nc.gpsimd, 0, j)
            for j in range(GROUP):
                split_dn_lo(pool, nc.gpsimd, 0, j)

        @block.scalar
        def _(act):
            def step(s, q, r, first=False, last=False):
                very_first, very_last = (isinstance(s, int) and s == n for n in (0, STEPS - 1))
                for j in range(GROUP):
                    n = GROUP * s + j
                    act.wait_ge(gate_done, n + 1)
                    wait(act, hidden_done, n - 1)
                    nc.scalar.activation(silu[:, j % 2], ps_gate[j % 2][:], ACT.Silu).then_inc(silu_done, 1)
                    act.wait_ge(hidden_done, n + 1)
                    nc.scalar.activation(hidden_abs[:, j], hidden[:, j], ACT.Abs).then_inc(abs_done, 1)
                    if last:
                        split_gu_hi(act, q + 1, j)
                    if very_first and j == 1:
                        split_x_hi(act, 1)
                if very_last:
                    wait(act, up_done, GROUP * STEPS)
                elif not very_first:
                    split_x_hi(act, s + 1)
                    wait(act, y_done, TILES * s)
                for j in range(GROUP):
                    act.wait_ge(kept_done, GROUP * s + j + 1)
                    nc.scalar.activation((x_hi if very_last else h_hi)[:, j], hidden[:, j],
                                         ACT.Copy).then_inc(h_hi_done, 1)
                if first:
                    if very_first:
                        act.wait_ge(up_done, GROUP)
                    for j in range(GROUP):
                        split_dn_hi(act, q, j)

            steps(act, step)

        @block.vector
        def _(dve):
            def compare(s, i, j):
                dve.wait_ge(abs_done, GROUP * s + j + 1)
                return nc.vector.tensor_tensor(beats[:, PAIR[i, j]], hidden_abs[:, i], hidden_abs[:, j], ALU.is_ge)

            def add_y(s, r, tiles=range(TILES)):
                for t in tiles:
                    dve.wait_ge(y_done, TILES * s + t + 1)
                    row = rows[:, bass.ds((TILES * r + t) * D, D)]
                    nc.vector.scalar_tensor_tensor(row, ps_y[t][:], ffn_gate[:], row, ALU.mult,
                                                   ALU.add).then_inc(y_added, 1)

            def step(s, q, r, first=False, last=False):
                very_first, very_last = (isinstance(s, int) and s == n for n in (0, STEPS - 1))
                for j in range(GROUP):
                    n = GROUP * s + j
                    wait(dve, h_lo_done, n - GROUP + 1)
                    dve.wait_ge(silu_done, n + 1)
                    dve.wait_ge(up_done, n + 1)
                    nc.vector.tensor_tensor(hidden[:, j], ps_up[j % 2][:], silu[:, j % 2], ALU.mult).then_inc(hidden_done, 1)
                    for i in range(j - 1):
                        compare(s, i, j - 1)
                    if last:
                        split_gu_lo(dve, nc.vector, q + 1, j)
                    if very_first and j == 1:
                        split_x_lo(dve, 1)
                if not very_first and not very_last:
                    split_x_lo(dve, s + 1)
                for i in range(GROUP - 1):
                    compared = compare(s, i, GROUP - 1)
                compared.then_inc(beats_done, 1)
                dve.wait_ge(beats_done, s + 1)
                nc.vector.tensor_tensor(part[:, 0:2], beats[:, 2:4], beats[:, 0:2], ALU.subtract)
                nc.vector.tensor_tensor(part[:, 2], beats[:, PAIR[0, 1]], beats[:, PAIR[0, 2]], ALU.add)
                nc.vector.tensor_tensor(part[:, 3], beats[:, PAIR[1, 3]], beats[:, PAIR[2, 3]], ALU.add).then_inc(part_done, 1)
                dve.wait_ge(part_done, s + 1)
                nc.vector.tensor_tensor(wins[:, 0:2], part[:, 0:2],
                                        beats[:, PAIR[1, 2]:PAIR[1, 2] + 1].to_broadcast([P, 2, ROWS]), ALU.add)
                nc.vector.tensor_tensor(wins[:, 2:4], part[:, 2:4],
                                        beats[:, PAIR[0, 3]:PAIR[0, 3] + 1].to_broadcast([P, 2, ROWS]),
                                        ALU.add).then_inc(wins_done, 1)
                dve.wait_ge(wins_done, s + 1)
                for j in range(GROUP):
                    at, test, bound = KEEP[j]
                    nc.vector.scalar_tensor_tensor(hidden[:, j], wins[:, at], bound, hidden[:, j], test,
                                                   ALU.mult).then_inc(kept_done, 1)
                def take_lower_parts(hi, lo):
                    for j in range(GROUP):
                        dve.wait_ge(h_hi_done, GROUP * s + j + 1)
                        nc.vector.tensor_tensor(lo[:, j], hidden[:, j], hi[:, j].bitcast(F32),
                                                ALU.subtract).then_inc(h_lo_done, 1)

                if very_last:
                    add_y(s - 1, r - 1, [0])
                    take_lower_parts(x_hi, x_lo)
                    add_y(s - 1, r - 1, range(1, TILES))
                else:
                    if not very_first:
                        add_y(s - 1, BLOCKS - 1 if first else r - 1)
                    take_lower_parts(h_hi, h_lo)
                if first and not very_first:
                    for j in range(GROUP):
                        split_dn_lo(dve, nc.vector, q, j)

            for c in range(KC // 2, KC):
                split_first_x_lo(dve, c)
            steps(dve, step)
            add_y(STEPS - 1, BLOCKS - 1)

        @block.tensor
        def _(pe):
            def three_products(bank, a_hi, a_lo, b_hi, b_lo, start, stop):
                nc.tensor.matmul(bank, a_hi, b_hi, start=start, stop=False)
                nc.tensor.matmul(bank, a_hi, b_lo, start=False, stop=False)
                return nc.tensor.matmul(bank, a_lo, b_hi, start=False, stop=stop)

            def gate_up(s, q=None, b_hi=x_hi, b_lo=x_lo):
                for j in range(GROUP):
                    n = GROUP * s + j
                    if q is not None:
                        pe.wait_ge(gu_lo_done, 2 * GROUP * q + 2 * j + 1)
                    wait(pe, silu_done, n - 1)
                    for c in range(KC):
                        if j == 0:
                            pe.wait_ge(x_lo_done, KC * s + c + 1)
                        last = three_products(ps_gate[j % 2][:], gu_hi[:, 0, j, c], gu_lo[:, 0, j, c],
                                              b_hi[:, c], b_lo[:, c], c == 0, c == KC - 1)
                    last.then_inc(gate_done, 1)
                    if q is not None:
                        pe.wait_ge(gu_lo_done, 2 * GROUP * q + 2 * j + 2)
                    wait(pe, hidden_done, n - 1)
                    for c in range(KC):
                        last = three_products(ps_up[j % 2][:], gu_hi[:, 1, j, c], gu_lo[:, 1, j, c],
                                              b_hi[:, c], b_lo[:, c], c == 0, c == KC - 1)
                    last.then_inc(up_done, 1)

            def down(s, q=None, hi=h_hi, lo=h_lo):
                if q is not None:
                    pe.wait_ge(dn_lo_done, GROUP * (q + 1))
                for t in range(TILES):
                    if hi is x_hi:
                        pe.wait_ge(y_added, TILES * (s - 1) + t + 1)
                    for j in range(GROUP):
                        if t == 0:
                            pe.wait_ge(h_lo_done, GROUP * s + j + 1)
                        at = slice(t * P, (t + 1) * P)
                        last = three_products(ps_y[t][:], hi[:, j, at], lo[:, j, at], dn_hi[:, j], dn_lo[:, j],
                                              j == 0, j == GROUP - 1)
                    last.then_inc(y_done, 1)

            def step(s, q, r, first=False, last=False):
                if isinstance(s, int) and s == 0:
                    gate_up(0, 0, dn_hi, dn_lo)
                    return
                gate_up(s, q if first else None)
                if not first:
                    down(s - 1, q if not isinstance(r, int) or r == 1 else None)
                else:
                    down(s - 1)

            steps(pe, step)
            down(STEPS - 1, hi=x_hi, lo=x_lo)


INS = ["x", "ctx_2048", "mask_BxS2_bk0", "g_xattn", "g_ffn", "L0_ffn_w_gate", "L0_ffn_w_up", "L0_ffn_w_down"]


def kernel(**inputs):
    import numpy as np
    import concourse.bacc as bacc
    from concourse.bass_utils import run_bass_kernel_spmd as run

    nc = bacc.Bacc("TRN2", target_bir_lowering=False, num_devices=1)
    arrays, args = {}, []
    for name in INS:
        a = np.ascontiguousarray(inputs[name])
        arrays[f"in_{name}"] = a
        args.append(nc.dram_tensor(f"in_{name}", a.shape, mybir.dt.from_np(a.dtype), kind="ExternalInput").ap())
    args.append(nc.dram_tensor("out_rows", (B, S, D), F32, kind="ExternalOutput").ap())
    flamingo_gated(nc, *args)
    r = run(nc, [arrays], core_ids=[0])
    return r.results[0]["out_rows"]
```

```python
from contextlib import ExitStack

import concourse.bass as bass
from concourse import mybir

F32 = mybir.dt.float32
F32R = mybir.dt.float32r
BF16 = mybir.dt.bfloat16
U8 = mybir.dt.uint8
ALU = mybir.AluOpType
ACT = mybir.ActivationFunctionType
AX = mybir.AxisListType

P = 128
B, S, D = 32, 128, 512
M = 128
I = 2048
KC = D // P
GROUP = 4
PASSES = I // (P * GROUP)
IQ = I // PASSES
ROWS = 512
TILES = ROWS // P
BLOCKS = B * S // ROWS
EPS = 1e-5
SCALE = float(D) ** -0.5
BIG = 1e30
RING = 8
LAST_LAG = 7
CONVERT = {1: (0,), 2: (1,), 3: (2, 3)}
VALID = {1: (0,), 2: (1,), 3: (2, 3)}
FIRST_X = {1: (0, 1), 2: (2, 3)}
FIRST_GU = {0: (0,), 3: (1,), 4: (2,), 5: (3,)}
KEEP = {0: (2, ALU.is_ge, 2.0), 1: (0, ALU.is_ge, 1.0), 2: (1, ALU.is_le, 0.0), 3: (3, ALU.is_le, 1.0)}
PAIR = {(0, 1): 0, (2, 3): 1, (1, 3): 2, (0, 2): 3, (1, 2): 4, (0, 3): 5}


def wait(engine, semaphore, value):
    if not isinstance(value, int) or value > 0:
        engine.wait_ge(semaphore, value)


def wait_apart(engine, semaphore, value, started):
    if isinstance(value, int):
        wait(engine, semaphore, value)
        return
    engine.compute_val(value)
    engine.wait_ge(started, 1)
    engine.wait_ge(semaphore, value)


def three_products(nc, bank, a_hi, a_lo, b_hi, b_lo, start, stop):
    nc.tensor.matmul(bank, a_hi, b_hi, start=start, stop=False)
    nc.tensor.matmul(bank, a_hi, b_lo, start=False, stop=False)
    return nc.tensor.matmul(bank, a_lo, b_hi, start=False, stop=stop)


def flamingo_gated(nc, x, ctx, mask, g_xattn, g_ffn, w_gate, w_up, w_down, out):
    xnT_dram = nc.dram_tensor("xnT_scratch", [BLOCKS, P, KC, ROWS], F32).ap()
    gate_view = w_gate.rearrange("(c p) i -> p c i", p=P)
    up_view = w_up.rearrange("(c p) i -> p c i", p=P)
    down_view = w_down.rearrange("(q p j) n -> q p (j n)", p=P, j=GROUP)
    out_view = out.rearrange("b s d -> s b d")

    whole = ExitStack()
    with whole:
        def sb(name, shape, dtype, scope=whole):
            return scope.enter_context(nc.sbuf_tensor(name, shape, dtype))

        def sem(name, scope=whole):
            return scope.enter_context(nc.semaphore(name))

        rows = sb("rows", [P, B * D], F32)
        gu_hi = sb("gu_hi", [P, 2, GROUP, KC, P], F32R)
        gu_lo = sb("gu_lo", [P, 2, GROUP, KC, P], F32R)
        dn_hi = sb("dn_hi", [P, GROUP, D], F32R)
        dn_lo = sb("dn_lo", [P, GROUP, D], F32R)
        gu_raw = sb("gu_raw", [P, 2, KC, IQ], F32)
        dn_raw = gu_raw[:, 0]
        x_raw = sb("x_raw", [P, KC, ROWS], F32)
        ffn_gate = sb("ffn_gate", [P, 1], F32)
        ps_gate0 = whole.enter_context(nc.psum_tensor("ps_gate0", [P, ROWS], F32))

        x_loaded, x_hi_done, x_lo_done = sem("x_loaded"), sem("x_hi_done"), sem("x_lo_done")
        x1nT_free = [sem(f"x1nT_free{t}") for t in range(TILES)]
        gate_raw_loaded, up_raw_loaded, dn_raw_loaded = sem("gate_raw_loaded"), sem("up_raw_loaded"), sem("dn_raw_loaded")
        gu_hi_done, gu_lo_done = sem("gu_hi_done"), sem("gu_lo_done")
        dn_hi_done, dn_lo_done = sem("dn_hi_done"), sem("dn_lo_done")
        gate_done = sem("gate_done")

        def gu_raw_of(g, j):
            return gu_raw[:, g, :, j:IQ:GROUP]

        def split_gu_hi(act, q, j):
            act.wait_ge(gate_raw_loaded, 16 * (q + 1))
            act.wait_ge(up_raw_loaded, 16 * (q + 1))
            for g in range(2):
                nc.scalar.activation(gu_hi[:, g, j], gu_raw_of(g, j), ACT.Copy).then_inc(gu_hi_done, 1)

        def split_gu_lo(engine, instructions, q, j, which=range(2)):
            for g in which:
                engine.wait_ge(gu_hi_done, 2 * GROUP * q + 2 * j + g + 1)
                instructions.tensor_tensor(gu_lo[:, g, j], gu_raw_of(g, j), gu_hi[:, g, j].bitcast(F32),
                                        ALU.subtract).then_inc(gu_lo_done, 1)

        def split_dn_hi(act, q, j):
            act.wait_ge(dn_raw_loaded, 16 * (q + 1))
            nc.scalar.activation(dn_hi[:, j], dn_raw[:, j], ACT.Copy).then_inc(dn_hi_done, 1)

        def split_dn_lo(engine, instructions, q, j):
            engine.wait_ge(dn_hi_done, GROUP * q + j + 1)
            instructions.tensor_tensor(dn_lo[:, j], dn_raw[:, j], dn_hi[:, j].bitcast(F32),
                                    ALU.subtract).then_inc(dn_lo_done, 1)

        def split_first_x_hi(act, c):
            act.wait_ge(x_loaded, 16)
            nc.scalar.activation(dn_hi[:, c], x_raw[:, c], ACT.Copy).then_inc(x_hi_done, 1)

        def split_first_x_lo(dve, c):
            dve.wait_ge(x_hi_done, c + 1)
            nc.vector.tensor_tensor(dn_lo[:, c], x_raw[:, c], dn_hi[:, c].bitcast(F32),
                                    ALU.subtract).then_inc(x_lo_done, 1)

        def first_gate(pe, chunks):
            for c in chunks:
                pe.wait_ge(x_lo_done, c + 1)
                last = three_products(nc, ps_gate0[:], gu_hi[:, 0, 0, c], gu_lo[:, 0, 0, c], dn_hi[:, c], dn_lo[:, c],
                                      c == 0, c == KC - 1)
            if c == KC - 1:
                last.then_inc(gate_done, 1)

        attention(nc, sb, sem, x=x, ctx=ctx, mask=mask, g_xattn=g_xattn, g_ffn=g_ffn, rows=rows, gu_raw=gu_raw,
                  ffn_gate=ffn_gate, xnT_dram=xnT_dram, x_raw=x_raw, x_loaded=x_loaded, x1nT_free=x1nT_free,
                  gate_view=gate_view, up_view=up_view, gate_raw_loaded=gate_raw_loaded, up_raw_loaded=up_raw_loaded,
                  split_gu_hi=split_gu_hi, split_gu_lo=split_gu_lo, split_first_x_hi=split_first_x_hi,
                  split_first_x_lo=split_first_x_lo, first_gate=first_gate, gu_lo_done=gu_lo_done, ps_gate0=ps_gate0)
        feed_forward(nc, sb, sem, rows=rows, ffn_gate=ffn_gate, gu_raw=gu_raw, dn_raw=dn_raw, gu_hi=gu_hi,
                     gu_lo=gu_lo, dn_hi=dn_hi, dn_lo=dn_lo, xnT_dram=xnT_dram, out_view=out_view, x_raw=x_raw,
                     x1nT_free=x1nT_free, gate_view=gate_view, up_view=up_view, down_view=down_view,
                     gate_raw_loaded=gate_raw_loaded, up_raw_loaded=up_raw_loaded, dn_raw_loaded=dn_raw_loaded,
                     gu_lo_done=gu_lo_done, dn_lo_done=dn_lo_done, split_gu_hi=split_gu_hi, split_gu_lo=split_gu_lo,
                     split_dn_hi=split_dn_hi, split_dn_lo=split_dn_lo, x_loaded=x_loaded, x_hi_done=x_hi_done,
                     x_lo_done=x_lo_done, ps_gate0=ps_gate0, gate_done=gate_done)


def attention(nc, sb, sem, *, x, ctx, mask, g_xattn, g_ffn, rows, gu_raw, ffn_gate, xnT_dram, x_raw, x_loaded,
              x1nT_free, gate_view, up_view, gate_raw_loaded, up_raw_loaded, split_gu_hi, split_gu_lo,
              split_first_x_hi, split_first_x_lo, first_gate, gu_lo_done, ps_gate0):
    scope = ExitStack()
    with scope:
        def sbuf(name, shape, dtype=F32):
            return sb(name, shape, dtype, scope)

        def psum(name, shape):
            return scope.enter_context(nc.psum_tensor(name, shape, F32))

        def semaphore(name):
            return sem(name, scope)

        x1nT = sbuf("x1nT", [P, TILES, KC, P])
        x_in = sbuf("x_in", [P, RING, D])
        ctx_in = sbuf("ctx_in", [P, RING, D])
        xn = sbuf("xn", [P, 2, D])
        xnT = sbuf("xnT", [P, 2, KC, P])
        ctxT = sbuf("ctxT", [P, 2, KC, P])
        mask_in = x1nT[:, 0:B * M // (4 * D)].rearrange("p t c n -> p (t c n)").bitcast(U8)
        mask_neg = sbuf("mask_neg", [P, B * M], BF16)
        neg_scores = sbuf("neg_scores", [P, 2, M])
        neg_max = sbuf("neg_max", [P, RING])
        probs = sbuf("probs", [P, 2, M])
        probsT = sbuf("probsT", [P, 2, P])
        prob_sum = sbuf("prob_sum", [P, RING])
        inv_sum = sbuf("inv_sum", [P, RING])
        out_scale = sbuf("out_scale", [P, RING])
        x1n = sbuf("x1n", [P, 2, D])
        bn6 = sbuf("bn6", [P, 2, 2, 6])
        bn_mv = sbuf("bn_mv", [P, 2, RING, 2])
        var_eps = sbuf("var_eps", [P, 2, RING])
        neg_mean = sbuf("neg_mean", [P, RING])
        neg_mean_rstd = sbuf("neg_mean_rstd", [P, RING])
        eps = sbuf("eps", [P, 1])
        minus_one = sbuf("minus_one", [P, 1])
        rstd = sbuf("rstd", [P, 2, RING])
        minus_half = sbuf("minus_half", [P, 1])
        xattn_gate = sbuf("xattn_gate", [P, 1])
        gates_in = sbuf("gates_in", [P, 2])
        valid = sbuf("valid", [P, B])
        gate_valid = sbuf("gate_valid", [P, B])
        ident = sbuf("ident", [P, P])

        ps_xT = ps_gate0[:].rearrange("p (c n) -> p c n", c=KC)
        ps_cT = psum("ps_cT", [P, KC, P])
        ps_sc = [psum(f"ps_sc{i}", [P, 512]) for i in range(2)]
        ps_pT = psum("ps_pT", [P, 512])
        ps_av = [psum(f"ps_av{i}", [P, D]) for i in range(2)]
        ps_nT = psum("ps_nT", [P, KC, P])

        x_in_loaded = [semaphore(f"x_in_loaded{k}") for k in range(RING)]
        ctx_in_loaded = [semaphore(f"ctx_in_loaded{k}") for k in range(RING)]
        gates_loaded, mask_loaded = semaphore("gates_loaded"), semaphore("mask_loaded")
        neg_mean_done, shift_done = semaphore("neg_mean_done"), semaphore("shift_done")
        ident_set, ident_done, half_done = semaphore("ident_set"), semaphore("ident_done"), semaphore("half_done")
        gates_done, valid_done, gate_valid_done = semaphore("gates_done"), semaphore("valid_done"), semaphore("gate_valid_done")
        bn1_done, stats1_done = semaphore("bn1_done"), semaphore("stats1_done")
        bn2_done, stats2_done = semaphore("bn2_done"), semaphore("stats2_done")
        var_eps_done = [semaphore(f"var_eps{i}_done") for i in (1, 2)]
        rstd_done = [semaphore(f"rstd{i}_done") for i in (1, 2)]
        xn_done, x1n_done = semaphore("xn_done"), semaphore("x1n_done")
        xT_done, cT_done, xT_copied, cT_copied = (semaphore(n) for n in ("xT_done", "cT_done", "xT_copied", "cT_copied"))
        scores_done, neg_scores_done, neg_max_done = (
            semaphore(n) for n in ("scores_done", "neg_scores_done", "neg_max_done"))
        probs_done, pT_done, pT_copied = semaphore("probs_done"), semaphore("pT_done"), semaphore("pT_copied")
        av_done, x1_done = semaphore("av_done"), semaphore("x1_done")
        inv_sum_done, out_scale_done = semaphore("inv_sum_done"), semaphore("out_scale_done")
        nT_done, nT_copied = semaphore("nT_done"), semaphore("nT_copied")

        def slots(engine, slot):
            def at_of(it, k):
                def at(lag):
                    r, kk = it + (k - lag) // RING, (k - lag) % RING
                    if isinstance(r, int) and not 0 <= r < B // RING:
                        return None
                    return r, kk
                return at
            for k in range(RING):
                slot(at_of(0, k), 0, k)
            with engine.Fori(1, B // RING) as it:
                for k in range(RING):
                    slot(at_of(it, k), None, k)
            for k in range(LAST_LAG):
                slot(at_of(B // RING, k), B // RING, k)

        block = scope.enter_context(nc.Block())

        @block.sync
        def _(sp):
            def load(r, k):
                b = RING * r + k
                wait(sp, av_done, b - RING + 1)
                wait(sp, x1_done, b - RING + 1)
                sp.dma_start(x_in[:, k], x[bass.ds(b, 1)].rearrange("b s d -> (b s) d")).then_inc(x_in_loaded[k], 16)
                sp.dma_start(ctx_in[:, k], ctx[bass.ds(b, 1)].rearrange("b s d -> (b s) d")).then_inc(ctx_in_loaded[k], 16)

            def store(r, k):
                b = RING * r + k
                t = k % TILES
                sp.wait_ge(nT_copied, b + 1)
                sp.dma_start(xnT_dram[bass.ds(2 * r + k // TILES, 1), :, :, t * P:(t + 1) * P].rearrange("r p c n -> (r p) c n"),
                             x1nT[:, t]).then_inc(x1nT_free[t], 16)

            for k in range(RING):
                load(0, k)
                if k == 1:
                    sp.dma_start(mask_in, mask.rearrange("b m -> (b m)").rearrange("(a n) -> a n", a=1)
                                 .to_broadcast([P, B * M])).then_inc(mask_loaded, 16)
                    for n, g in enumerate((g_xattn, g_ffn)):
                        sp.dma_start(gates_in[:, n:n + 1], g.rearrange("(a n) -> a n", a=1)
                                     .to_broadcast([P, 1])).then_inc(gates_loaded, 16)
            ahead = 2
            for k in range(ahead):
                load(1, k)
            sp.dma_start(gu_raw[:, 0], gate_view[:, :, 0:IQ]).then_inc(gate_raw_loaded, 16)
            sp.dma_start(gu_raw[:, 1], up_view[:, :, 0:IQ]).then_inc(up_raw_loaded, 16)
            with sp.Fori(1, B // RING - 1) as r:
                for k in range(RING):
                    store(r - 1, k)
                    load(r + (k + ahead) // RING, (k + ahead) % RING)
            for k in range(RING):
                store(B // RING - 2, k)
                if k + ahead < RING:
                    load(B // RING - 1, k + ahead)
            for t in range(TILES):
                sp.wait_ge(x1nT_free[t], 16 * 2)
            sp.dma_start(x_raw[:].rearrange("p c n -> p (c n)"),
                         xnT_dram[0].rearrange("p c n -> p (c n)")).then_inc(x_loaded, 16)
            for k in range(RING):
                store(B // RING - 1, k)

        @block.gpsimd
        def _(pool):
            nc.gpsimd.memset(eps[:], EPS)
            nc.gpsimd.memset(minus_one[:], -1.0)
            nc.gpsimd.memset(minus_half[:], -0.5).then_inc(half_done, 1)
            nc.gpsimd.memset(ident[:], 0.0).then_inc(ident_set, 1)
            pool.wait_ge(ident_set, 1)
            nc.gpsimd.affine_select(out=ident[:], in_=ident[:], compare_op=ALU.not_equal, fill=1.0, base=0,
                                    pattern=[[-1, P]], channel_multiplier=1).then_inc(ident_done, 1)
            pool.wait_ge(half_done, 1)

            def inverse_deviation(which, k, b):
                pool.wait_ge((stats1_done, stats2_done)[which], b + 1)
                nc.gpsimd.tensor_tensor(var_eps[:, which, k:k + 1], bn_mv[:, which, k, 1:2], eps[:],
                                        ALU.add).then_inc(var_eps_done[which], 1)
                if which == 0:
                    nc.gpsimd.tensor_tensor(neg_mean[:, k:k + 1], bn_mv[:, 0, k, 0:1], minus_one[:],
                                            ALU.mult).then_inc(neg_mean_done, 1)
                pool.wait_ge(var_eps_done[which], b + 1)
                nc.gpsimd.tensor_tensor(rstd[:, which, k:k + 1], var_eps[:, which, k:k + 1], minus_half[:],
                                        ALU.pow).then_inc(rstd_done[which], 1)

            def slot(at, it, k0):
                if at(6) is not None:
                    r, k = at(6)
                    inverse_deviation(1, k, RING * r + k)
                if at(0) is not None:
                    r, k = at(0)
                    b = RING * r + k
                    inverse_deviation(0, k, b)
                    pool.wait_ge(neg_mean_done, b + 1)
                    pool.wait_ge(rstd_done[0], b + 1)
                    nc.gpsimd.tensor_tensor(neg_mean_rstd[:, k:k + 1], neg_mean[:, k:k + 1], rstd[:, 0, k:k + 1],
                                            ALU.mult).then_inc(shift_done, 1)
                if at(4) is not None:
                    r, k = at(4)
                    b = RING * r + k
                    pool.wait_ge(probs_done, b + 1)
                    nc.gpsimd.tensor_tensor(inv_sum[:, k:k + 1], prob_sum[:, k:k + 1], minus_one[:],
                                            ALU.pow).then_inc(inv_sum_done, 1)
                    if isinstance(b, int) and b == 0:
                        pool.wait_ge(gate_valid_done, 1)
                    wait_apart(pool, inv_sum_done, b + 1, half_done)
                    nc.gpsimd.tensor_tensor(out_scale[:, k:k + 1], inv_sum[:, k:k + 1], gate_valid[:, bass.ds(b, 1)],
                                            ALU.mult).then_inc(out_scale_done, 1)
                if it == B // RING and k0 in (4, 5):
                    split_gu_lo(pool, nc.gpsimd, 0, 0, [k0 - 4])
                if it == 0 and k0 in CONVERT:
                    pool.wait_ge(mask_loaded, 16)
                    for at_m in CONVERT[k0]:
                        part = slice(at_m * RING * M, (at_m + 1) * RING * M)
                        nc.gpsimd.tensor_scalar(mask_neg[:, part], mask_in[:, part], -BIG, BIG, ALU.mult,
                                                ALU.add).then_inc(x1nT_free[at_m], 16)

            slots(pool, slot)

        @block.scalar
        def _(act):
            def slot(at, it, k0):
                if at(1) is not None:
                    r, k = at(1)
                    b = RING * r + k
                    wait(act, scores_done, b - 1)
                    act.wait_ge(cT_done, b + 1)
                    nc.scalar.activation(ctxT[:, k % 2], ps_cT[:], ACT.Copy).then_inc(cT_copied, 1)
                    act.wait_ge(xT_done, b + 1)
                    nc.scalar.activation(xnT[:, k % 2], ps_xT, ACT.Copy).then_inc(xT_copied, 1)
                if at(3) is not None:
                    r, k = at(3)
                    b = RING * r + k
                    act.wait_ge(neg_max_done, b + 1)
                    wait(act, pT_done, b - 1)
                    nc.scalar.activation(probs[:, k % 2], neg_scores[:, k % 2], ACT.Exp, bias=neg_max[:, k:k + 1],
                                         scale=-1.0, accum_out=prob_sum[:, k:k + 1]).then_inc(probs_done, 1)
                if at(0) is not None:
                    r, k = at(0)
                    b = RING * r + k
                    wait(act, xT_done, b - 1)
                    act.wait_ge(shift_done, b + 1)
                    nc.scalar.activation(xn[:, k % 2], x_in[:, k], ACT.Identity, bias=neg_mean_rstd[:, k:k + 1],
                                         scale=rstd[:, 0, k:k + 1]).then_inc(xn_done, 1)
                if at(7) is not None:
                    r, k = at(7)
                    b = RING * r + k
                    t = k % TILES
                    act.wait_ge(x1nT_free[t], 16 * (2 * r + k // TILES + 1))
                    act.wait_ge(nT_done, b + 1)
                    nc.scalar.activation(x1nT[:, t], ps_nT[:], ACT.Copy).then_inc(nT_copied, 1)
                if at(3) is not None:
                    r, k = at(3)
                    b = RING * r + k
                    act.wait_ge(pT_done, b + 1)
                    wait(act, av_done, b - 1)
                    nc.scalar.activation(probsT[:, k % 2], ps_pT[:, 0:P], ACT.Copy).then_inc(pT_copied, 1)
                if it == 0 and k0 == 1:
                    act.wait_ge(gates_loaded, 32)
                    nc.scalar.activation(xattn_gate[:], gates_in[:, 0:1], ACT.Tanh).then_inc(gates_done, 1)
                    nc.scalar.activation(ffn_gate[:], gates_in[:, 1:2], ACT.Tanh).then_inc(gates_done, 1)
                if it == B // RING:
                    for c in FIRST_X.get(k0, ()):
                        split_first_x_hi(act, c)
                    for j in FIRST_GU.get(k0, ()):
                        split_gu_hi(act, 0, j)

            slots(act, slot)

        @block.vector
        def _(dve):
            def slot(at, it, k0):
                if at(0) is not None:
                    r, k = at(0)
                    b = RING * r + k
                    dve.wait_ge(x_in_loaded[k], 16 * (r + 1))
                    nc.vector.bn_stats(bn6[:, 0, k % 2], x_in[:, k]).then_inc(bn1_done, 1)
                if at(6) is not None:
                    r, k = at(6)
                    wait_apart(dve, bn2_done, RING * r + k + 1, bn1_done)
                    nc.vector.bn_aggr(bn_mv[:, 1, k], bn6[:, 1, k % 2]).then_inc(stats2_done, 1)
                if at(0) is not None:
                    r, k = at(0)
                    wait_apart(dve, bn1_done, RING * r + k + 1, bn1_done)
                    nc.vector.bn_aggr(bn_mv[:, 0, k], bn6[:, 0, k % 2]).then_inc(stats1_done, 1)
                if it == 0 and k0 in VALID:
                    dve.wait_ge(mask_loaded, 16)
                    for n in VALID[k0]:
                        nc.vector.tensor_reduce(valid[:, n * RING:(n + 1) * RING],
                                                mask_in[:, n * RING * M:(n + 1) * RING * M]
                                                .rearrange("p (b m) -> p b m", m=M), AX.X, ALU.max).then_inc(valid_done, 1)
                if at(3) is not None:
                    r, k = at(3)
                    b = RING * r + k
                    wait(dve, probs_done, b - 1)
                    dve.wait_ge(scores_done, b + 1)
                    if isinstance(b, int) and b == 0:
                        dve.wait_ge(x1nT_free[0], 16)
                    if isinstance(b, int) and b == 2:
                        for t in range(1, TILES):
                            dve.wait_ge(x1nT_free[t], 16)
                    nc.vector.scalar_tensor_tensor(neg_scores[:, k % 2], ps_sc[k % 2][:, 0:M], -SCALE,
                                                   mask_neg[:, bass.ds(b * M, M)], ALU.mult, ALU.add).then_inc(neg_scores_done, 1)
                if at(3) is not None:
                    r, k = at(3)
                    dve.wait_ge(neg_scores_done, RING * r + k + 1)
                    nc.vector.tensor_reduce(neg_max[:, k:k + 1], neg_scores[:, k % 2], AX.X, ALU.min).then_inc(neg_max_done, 1)
                if at(5) is not None:
                    r, k = at(5)
                    b = RING * r + k
                    dve.wait_ge(out_scale_done, b + 1)
                    dve.wait_ge(av_done, b + 1)
                    nc.vector.scalar_tensor_tensor(rows[:, bass.ds(b * D, D)], ps_av[k % 2][:], out_scale[:, k:k + 1],
                                                   x_in[:, k], ALU.mult, ALU.add).then_inc(x1_done, 1)
                if at(6) is not None:
                    r, k = at(6)
                    b = RING * r + k
                    wait(dve, nT_done, b - 1)
                    if it == B // RING and k0 == 5:
                        split_first_x_lo(dve, 0)
                    dve.wait_ge(rstd_done[1], b + 1)
                    nc.vector.tensor_scalar(x1n[:, k % 2], rows[:, bass.ds(b * D, D)], bn_mv[:, 1, k, 0:1],
                                            rstd[:, 1, k:k + 1], ALU.subtract, ALU.mult).then_inc(x1n_done, 1)
                if at(5) is not None:
                    r, k = at(5)
                    b = RING * r + k
                    wait_apart(dve, x1_done, b + 1, bn1_done)
                    nc.vector.bn_stats(bn6[:, 1, k % 2], rows[:, bass.ds(b * D, D)]).then_inc(bn2_done, 1)
                if it == 0 and k0 == 3:
                    dve.wait_ge(valid_done, TILES)
                    dve.wait_ge(gates_done, 1)
                    nc.vector.tensor_scalar(gate_valid[:], valid[:], xattn_gate[:], None, ALU.mult).then_inc(gate_valid_done, 1)

            slots(dve, slot)
            for c in range(1, KC):
                split_first_x_lo(dve, c)

        @block.tensor
        def _(pe):
            pe.wait_ge(ident_done, 1)

            def slot(at, it, k0):
                if at(1) is not None:
                    r, k = at(1)
                    b = RING * r + k
                    pe.wait_ge(ctx_in_loaded[k], 16 * (r + 1))
                    wait(pe, cT_copied, b)
                    for c in range(KC):
                        last = nc.tensor.transpose(ps_cT[:, c], ctx_in[:, k, c * P:(c + 1) * P], ident[:])
                    last.then_inc(cT_done, 1)
                    pe.wait_ge(xn_done, b + 1)
                    wait(pe, xT_copied, b)
                    for c in range(KC):
                        last = nc.tensor.transpose(ps_xT[:, c], xn[:, k % 2, c * P:(c + 1) * P], ident[:])
                    last.then_inc(xT_done, 1)
                if at(2) is not None:
                    r, k = at(2)
                    b = RING * r + k
                    pe.wait_ge(xT_copied, b + 1)
                    pe.wait_ge(cT_copied, b + 1)
                    wait(pe, neg_scores_done, b - 1)
                    for c in range(KC):
                        last = nc.tensor.matmul(ps_sc[k % 2][:, 0:M], xnT[:, k % 2, c], ctxT[:, k % 2, c],
                                                start=(c == 0), stop=(c == KC - 1))
                    last.then_inc(scores_done, 1)
                if at(7) is not None:
                    r, k = at(7)
                    b = RING * r + k
                    pe.wait_ge(x1n_done, b + 1)
                    wait(pe, nT_copied, b)
                    for c in range(KC):
                        last = nc.tensor.transpose(ps_nT[:, c], x1n[:, k % 2, c * P:(c + 1) * P], ident[:])
                    last.then_inc(nT_done, 1)
                if it == B // RING and k0 == 5:
                    pe.wait_ge(xT_copied, B)
                    pe.wait_ge(gu_lo_done, 1)
                    first_gate(pe, [0])
                if at(4) is not None:
                    r, k = at(4)
                    b = RING * r + k
                    pe.wait_ge(pT_copied, b + 1)
                    wait(pe, x1_done, b - 1)
                    nc.tensor.matmul(ps_av[k % 2][:], probsT[:, k % 2], ctx_in[:, k], start=True,
                                     stop=True).then_inc(av_done, 1)
                if at(3) is not None:
                    r, k = at(3)
                    b = RING * r + k
                    pe.wait_ge(probs_done, b + 1)
                    wait(pe, pT_copied, b)
                    nc.tensor.transpose(ps_pT[:, 0:P], probs[:, k % 2], ident[:]).then_inc(pT_done, 1)

            slots(pe, slot)
            first_gate(pe, range(1, KC))


def feed_forward(nc, sb, sem, *, rows, ffn_gate, gu_raw, dn_raw, gu_hi, gu_lo, dn_hi, dn_lo, xnT_dram, out_view,
                 x_raw, x1nT_free, gate_view, up_view, down_view, gate_raw_loaded, up_raw_loaded, dn_raw_loaded,
                 gu_lo_done, dn_lo_done, split_gu_hi, split_gu_lo, split_dn_hi, split_dn_lo, x_loaded, x_hi_done,
                 x_lo_done, ps_gate0, gate_done):
    STEPS = PASSES * BLOCKS

    scope = ExitStack()
    with scope:
        def sbuf(name, shape, dtype=F32):
            return sb(name, shape, dtype, scope)

        def psum(name, shape):
            return scope.enter_context(nc.psum_tensor(name, shape, F32))

        def semaphore(name):
            return sem(name, scope)

        h_lo = sbuf("h_lo", [P, GROUP, ROWS], F32R)
        x_hi = sbuf("x_hi", [P, KC, ROWS], F32R)
        x_lo = sbuf("x_lo", [P, KC, ROWS], F32R)
        silu = sbuf("silu", [P, 2, ROWS])
        hidden = sbuf("hidden", [P, GROUP, ROWS])
        hidden_abs = sbuf("hidden_abs", [P, GROUP, ROWS])
        beats = sbuf("beats", [P, 6, ROWS], BF16)
        part = sbuf("part", [P, 4, ROWS], BF16)
        wins = sbuf("wins", [P, 4, ROWS], BF16)
        h_hi = sbuf("h_hi", [P, GROUP, ROWS], F32R)

        ps_gate = [ps_gate0, psum("ps_gate1", [P, ROWS])]
        ps_up = [psum(f"ps_up{i}", [P, ROWS]) for i in range(2)]
        ps_y = [psum(f"ps_y{i}", [P, D]) for i in range(TILES)]

        up_done, silu_done = semaphore("up_done"), semaphore("silu_done")
        hidden_done, abs_done, beats_done = semaphore("hidden_done"), semaphore("abs_done"), semaphore("beats_done")
        part_done, wins_done, kept_done = semaphore("part_done"), semaphore("wins_done"), semaphore("kept_done")
        h_hi_done, h_lo_done = semaphore("h_hi_done"), semaphore("h_lo_done")
        y_done, y_added, stored = semaphore("y_done"), semaphore("y_added"), semaphore("stored")

        def steps(engine, step):
            step(0, 0, 0, first=True)
            with engine.Fori(0, PASSES - 1) as q:
                with engine.Fori(1, BLOCKS - 1) as r:
                    step(q * BLOCKS + r, q, r)
                step(q * BLOCKS + BLOCKS - 1, q, BLOCKS - 1, last=True)
                step(q * BLOCKS + BLOCKS, q + 1, 0, first=True)
            q = PASSES - 1
            with engine.Fori(1, BLOCKS - 1) as r:
                step(q * BLOCKS + r, q, r)
            step(q * BLOCKS + BLOCKS - 1, q, BLOCKS - 1)

        block = scope.enter_context(nc.Block())

        @block.sync
        def _(sp):
            def load_x(s, r):
                wait(sp, x_hi_done, KC * s)
                wait(sp, x_lo_done, KC * s)
                sp.dma_start(x_raw[:].rearrange("p c n -> p (c n)"),
                             xnT_dram[bass.ds(r, 1)].rearrange("r p c n -> (r p) (c n)")).then_inc(x_loaded, 16)

            def load_gu_raw(q):
                sp.wait_ge(dn_lo_done, GROUP * q)
                sp.dma_start(gu_raw[:, 0], gate_view[:, :, bass.ds(q * IQ, IQ)]).then_inc(gate_raw_loaded, 16)
                sp.dma_start(gu_raw[:, 1], up_view[:, :, bass.ds(q * IQ, IQ)]).then_inc(up_raw_loaded, 16)

            def load_dn_raw(q):
                sp.wait_ge(gu_lo_done, 2 * GROUP * (q + 1))
                sp.dma_start(dn_raw.rearrange("p c n -> p (c n)"),
                             down_view[bass.ds(q, 1)].rearrange("q p n -> (q p) n")).then_inc(dn_raw_loaded, 16)

            def store_block(s, r):
                sp.wait_ge(y_added, TILES * (s + 1))
                sp.dma_start(out_view[:, bass.ds(r * TILES, TILES), :],
                             rows[:, bass.ds(r * TILES * D, TILES * D)].rearrange("p (b d) -> p b d", d=D)
                             ).then_inc(stored, 16)

            for t in range(TILES):
                sp.wait_ge(x1nT_free[t], 16 * (1 + BLOCKS))
            with sp.Fori(0, PASSES - 1) as q:
                load_x(q * BLOCKS + 1, 1)
                load_dn_raw(q)
                load_gu_raw(q + 1)
                with sp.Fori(2, BLOCKS) as r:
                    load_x(q * BLOCKS + r, r)
                load_x(q * BLOCKS + BLOCKS, 0)
            base = (PASSES - 1) * BLOCKS
            load_x(base + 1, 1)
            load_dn_raw(PASSES - 1)
            with sp.Fori(2, BLOCKS) as r:
                load_x(base + r, r)
                store_block(base + r - 2, r - 2)
            store_block(STEPS - 2, BLOCKS - 2)
            for t in range(TILES):
                sp.wait_ge(y_added, TILES * (STEPS - 1) + t + 1)
                at = (BLOCKS - 1) * TILES + t
                sp.dma_start(out_view[:, at], rows[:, at * D:(at + 1) * D]).then_inc(stored, 16)
            sp.wait_ge(stored, 16 * (BLOCKS - 1 + TILES))

        def split_x_hi(act, s):
            act.wait_ge(x_loaded, 16 * (s + 1))
            if not isinstance(s, int) or s > 1:
                wait(act, up_done, GROUP * s)
            for c in range(KC):
                nc.scalar.activation(x_hi[:, c], x_raw[:, c], ACT.Copy).then_inc(x_hi_done, 1)

        def split_x_lo(dve, s):
            for c in range(KC):
                dve.wait_ge(x_hi_done, KC * s + c + 1)
                nc.vector.tensor_tensor(x_lo[:, c], x_raw[:, c], x_hi[:, c].bitcast(F32),
                                        ALU.subtract).then_inc(x_lo_done, 1)

        @block.gpsimd
        def _(pool):
            for j in range(1, GROUP):
                split_gu_lo(pool, nc.gpsimd, 0, j)
            for j in range(GROUP):
                split_dn_lo(pool, nc.gpsimd, 0, j)

        @block.scalar
        def _(act):
            def step(s, q, r, first=False, last=False):
                very_first, very_last = (isinstance(s, int) and s == n for n in (0, STEPS - 1))
                for j in range(GROUP):
                    n = GROUP * s + j
                    act.wait_ge(gate_done, n + 1)
                    wait(act, hidden_done, n - 1)
                    nc.scalar.activation(silu[:, j % 2], ps_gate[j % 2][:], ACT.Silu).then_inc(silu_done, 1)
                    act.wait_ge(hidden_done, n + 1)
                    nc.scalar.activation(hidden_abs[:, j], hidden[:, j], ACT.Abs).then_inc(abs_done, 1)
                    if last:
                        split_gu_hi(act, q + 1, j)
                    if very_first and j == 1:
                        split_x_hi(act, 1)
                if very_last:
                    wait(act, up_done, GROUP * STEPS)
                elif not very_first:
                    split_x_hi(act, s + 1)
                    wait(act, y_done, TILES * s)
                if very_first:
                    act.wait_ge(up_done, GROUP)
                    for j in range(GROUP):
                        split_dn_hi(act, q, j)
                for j in range(GROUP):
                    act.wait_ge(kept_done, GROUP * s + j + 1)
                    nc.scalar.activation((x_hi if very_last else h_hi)[:, j], hidden[:, j],
                                         ACT.Copy).then_inc(h_hi_done, 1)
                if first and not very_first:
                    for j in range(GROUP):
                        split_dn_hi(act, q, j)

            steps(act, step)

        @block.vector
        def _(dve):
            def compare(s, i, j):
                dve.wait_ge(abs_done, GROUP * s + j + 1)
                return nc.vector.tensor_tensor(beats[:, PAIR[i, j]], hidden_abs[:, i], hidden_abs[:, j], ALU.is_ge)

            def add_y(s, r, tiles=range(TILES)):
                for t in tiles:
                    dve.wait_ge(y_done, TILES * s + t + 1)
                    row = rows[:, bass.ds((TILES * r + t) * D, D)]
                    nc.vector.scalar_tensor_tensor(row, ps_y[t][:], ffn_gate[:], row, ALU.mult,
                                                   ALU.add).then_inc(y_added, 1)

            def step(s, q, r, first=False, last=False):
                very_first, very_last = (isinstance(s, int) and s == n for n in (0, STEPS - 1))
                for j in range(GROUP):
                    n = GROUP * s + j
                    wait(dve, h_lo_done, n - GROUP + 1)
                    dve.wait_ge(silu_done, n + 1)
                    dve.wait_ge(up_done, n + 1)
                    nc.vector.tensor_tensor(hidden[:, j], ps_up[j % 2][:], silu[:, j % 2], ALU.mult).then_inc(hidden_done, 1)
                    for i in range(j - 1):
                        compare(s, i, j - 1)
                    if last:
                        split_gu_lo(dve, nc.vector, q + 1, j)
                    if very_first and j == 1:
                        split_x_lo(dve, 1)
                if not very_first and not very_last:
                    split_x_lo(dve, s + 1)
                for i in range(GROUP - 1):
                    compared = compare(s, i, GROUP - 1)
                compared.then_inc(beats_done, 1)
                dve.wait_ge(beats_done, s + 1)
                nc.vector.tensor_tensor(part[:, 0:2], beats[:, 2:4], beats[:, 0:2], ALU.subtract)
                nc.vector.tensor_tensor(part[:, 2], beats[:, PAIR[0, 1]], beats[:, PAIR[0, 2]], ALU.add)
                nc.vector.tensor_tensor(part[:, 3], beats[:, PAIR[1, 3]], beats[:, PAIR[2, 3]], ALU.add).then_inc(part_done, 1)
                dve.wait_ge(part_done, s + 1)
                nc.vector.tensor_tensor(wins[:, 0:2], part[:, 0:2],
                                        beats[:, PAIR[1, 2]:PAIR[1, 2] + 1].to_broadcast([P, 2, ROWS]), ALU.add)
                nc.vector.tensor_tensor(wins[:, 2:4], part[:, 2:4],
                                        beats[:, PAIR[0, 3]:PAIR[0, 3] + 1].to_broadcast([P, 2, ROWS]),
                                        ALU.add).then_inc(wins_done, 1)
                dve.wait_ge(wins_done, s + 1)
                for j in range(GROUP):
                    at, test, bound = KEEP[j]
                    nc.vector.scalar_tensor_tensor(hidden[:, j], wins[:, at], bound, hidden[:, j], test,
                                                   ALU.mult).then_inc(kept_done, 1)
                def take_lower_parts(hi, lo):
                    for j in range(GROUP):
                        dve.wait_ge(h_hi_done, GROUP * s + j + 1)
                        nc.vector.tensor_tensor(lo[:, j], hidden[:, j], hi[:, j].bitcast(F32),
                                                ALU.subtract).then_inc(h_lo_done, 1)

                if very_last:
                    add_y(s - 1, r - 1, [0])
                    take_lower_parts(x_hi, x_lo)
                    add_y(s - 1, r - 1, range(1, TILES))
                else:
                    if not very_first:
                        add_y(s - 1, BLOCKS - 1 if first else r - 1)
                    take_lower_parts(h_hi, h_lo)
                if first and not very_first:
                    for j in range(GROUP):
                        split_dn_lo(dve, nc.vector, q, j)

            steps(dve, step)
            add_y(STEPS - 1, BLOCKS - 1)

        @block.tensor
        def _(pe):
            def up(s, j, q, b_hi, b_lo):
                if q is not None:
                    pe.wait_ge(gu_lo_done, 2 * GROUP * q + 2 * j + 2)
                wait(pe, hidden_done, GROUP * s + j - 1)
                for c in range(KC):
                    last = three_products(nc, ps_up[j % 2][:], gu_hi[:, 1, j, c], gu_lo[:, 1, j, c],
                                          b_hi[:, c], b_lo[:, c], c == 0, c == KC - 1)
                last.then_inc(up_done, 1)

            def gate_up(s, q=None, b_hi=x_hi, b_lo=x_lo, gate_begun=False):
                for j in range(GROUP):
                    n = GROUP * s + j
                    if j == 0 and gate_begun:
                        up(s, j, q, b_hi, b_lo)
                        continue
                    if q is not None:
                        pe.wait_ge(gu_lo_done, 2 * GROUP * q + 2 * j + 1)
                    wait(pe, silu_done, n - 1)
                    for c in range(KC):
                        if j == 0:
                            pe.wait_ge(x_lo_done, KC * s + c + 1)
                        last = three_products(nc, ps_gate[j % 2][:], gu_hi[:, 0, j, c], gu_lo[:, 0, j, c],
                                              b_hi[:, c], b_lo[:, c], c == 0, c == KC - 1)
                    last.then_inc(gate_done, 1)
                    up(s, j, q, b_hi, b_lo)

            def down(s, q=None, hi=h_hi, lo=h_lo):
                if q is not None:
                    pe.wait_ge(dn_lo_done, GROUP * (q + 1))
                for t in range(TILES):
                    if hi is x_hi:
                        pe.wait_ge(y_added, TILES * (s - 1) + t + 1)
                    for j in range(GROUP):
                        if t == 0:
                            pe.wait_ge(h_lo_done, GROUP * s + j + 1)
                        at = slice(t * P, (t + 1) * P)
                        last = three_products(nc, ps_y[t][:], hi[:, j, at], lo[:, j, at], dn_hi[:, j], dn_lo[:, j],
                                              j == 0, j == GROUP - 1)
                    last.then_inc(y_done, 1)

            def step(s, q, r, first=False, last=False):
                if isinstance(s, int) and s == 0:
                    gate_up(0, 0, dn_hi, dn_lo, gate_begun=True)
                    return
                gate_up(s, q if first else None)
                if not first:
                    down(s - 1, q if not isinstance(r, int) or r == 1 else None)
                else:
                    down(s - 1)

            steps(pe, step)
            down(STEPS - 1, hi=x_hi, lo=x_lo)


INS = ["x", "ctx_2048", "mask_BxS2_bk0", "g_xattn", "g_ffn", "L0_ffn_w_gate", "L0_ffn_w_up", "L0_ffn_w_down"]


def kernel(**inputs):
    import numpy as np
    import concourse.bacc as bacc
    from concourse.bass_utils import run_bass_kernel_spmd as run

    nc = bacc.Bacc("TRN2", target_bir_lowering=False, num_devices=1)
    arrays, args = {}, []
    for name in INS:
        a = np.ascontiguousarray(inputs[name])
        arrays[f"in_{name}"] = a
        args.append(nc.dram_tensor(f"in_{name}", a.shape, mybir.dt.from_np(a.dtype), kind="ExternalInput").ap())
    args.append(nc.dram_tensor("out_rows", (B, S, D), F32, kind="ExternalOutput").ap())
    flamingo_gated(nc, *args)
    r = run(nc, [arrays], core_ids=[0])
    return r.results[0]["out_rows"]
```
